# Optimizing a Trainium2 kernel written in Bass

```python
import numpy as np
import jax
import jax.numpy as jnp

def _softmax(x, axis=-1):
    return jax.nn.softmax(x, axis=axis)

def _gelu(x):
    return jax.nn.gelu(x, approximate=True)

def _silu(x):
    return jax.nn.silu(x)

def _sigmoid(x):
    return jax.nn.sigmoid(x)

def _layernorm(x, axis=-1, eps=1e-05):
    m = jnp.mean(x, axis=axis, keepdims=True)
    v = jnp.var(x, axis=axis, keepdims=True)
    return (x - m) / jnp.sqrt(v + eps)

def _scatter_add(tgt, idx, src, axis=0):
    return tgt.at[idx].add(src)

def _segment_sum(src, seg, n):
    return jax.ops.segment_sum(src, seg, n)
kernel_name = 'mk_sandwich_d1_jaxref_r8_cf1b76'

def setup_inputs(seed: int=0):
    np.random.seed(seed)
    _w = jnp.asarray

    def _L0_attn_setup():
        import jax, jax.numpy as jnp
        import numpy as np
        BATCH, SEQ, D_MODEL, N_HEADS, D_HEAD = (2, 256, 256, 16, 128)
        ATTN_SCALE = np.sqrt(D_HEAD).astype(np.float32)
        IGNORE = jnp.float32(-100000.0)
        key = jax.random.key(seed)
        ks = jax.random.split(key, 5)
        init = 1.0 / np.sqrt(D_MODEL)
        return {'x': jax.random.normal(ks[0], (BATCH, SEQ, D_MODEL), jnp.float32), 'W_Q': jax.random.normal(ks[1], (N_HEADS, D_MODEL, D_HEAD), jnp.float32) * init, 'W_K': jax.random.normal(ks[2], (N_HEADS, D_MODEL, D_HEAD), jnp.float32) * init, 'W_V': jax.random.normal(ks[3], (N_HEADS, D_MODEL, D_HEAD), jnp.float32) * init, 'W_O': jax.random.normal(ks[4], (N_HEADS, D_HEAD, D_MODEL), jnp.float32) * init, 'b_Q': jnp.zeros((N_HEADS, D_HEAD), jnp.float32), 'b_K': jnp.zeros((N_HEADS, D_HEAD), jnp.float32), 'b_V': jnp.zeros((N_HEADS, D_HEAD), jnp.float32), 'b_O': jnp.zeros((D_MODEL,), jnp.float32)}
    _L0_attn_in = _L0_attn_setup()

    def _L0_ffn_setup():
        import jax, jax.numpy as jnp
        import numpy as np
        BLOCK_SIZE = 32
        HIDDEN_SIZE = 256
        MLP_DIM = 2048
        NVFP4_LUT = jnp.array([0.0, 0.5, 1.0, 1.5, 2.0, 3.0, 4.0, 6.0, 0.0, -0.5, -1.0, -1.5, -2.0, -3.0, -4.0, -6.0], dtype=jnp.float32)

        def dequant_nvfp4(W_packed, scales, block=BLOCK_SIZE):
            N = W_packed.shape[0]
            low = W_packed & 15
            high = W_packed >> 4 & 15
            idx = jnp.stack([low, high], axis=-1).reshape(N, -1)
            vals = NVFP4_LUT[idx]
            K = vals.shape[1]
            vals = vals.reshape(N, K // block, block) * scales[:, :, None]
            return vals.reshape(N, K)
        key = jax.random.key(seed)
        ks = jax.random.split(key, 7)
        x = jax.random.normal(ks[0], (4, 32, HIDDEN_SIZE), dtype=jnp.float32)
        gate_W_packed = jax.random.randint(ks[1], (MLP_DIM, HIDDEN_SIZE // 2), 0, 32, dtype=jnp.int32)
        gate_scales = jax.random.uniform(ks[2], (MLP_DIM, HIDDEN_SIZE // BLOCK_SIZE), dtype=jnp.float32) * 0.1 + 0.001
        up_W_packed = jax.random.randint(ks[3], (MLP_DIM, HIDDEN_SIZE // 2), 0, 32, dtype=jnp.int32)
        up_scales = jax.random.uniform(ks[4], (MLP_DIM, HIDDEN_SIZE // BLOCK_SIZE), dtype=jnp.float32) * 0.1 + 0.001
        down_W_packed = jax.random.randint(ks[5], (HIDDEN_SIZE, MLP_DIM // 2), 0, 32, dtype=jnp.int32)
        down_scales = jax.random.uniform(ks[6], (HIDDEN_SIZE, MLP_DIM // BLOCK_SIZE), dtype=jnp.float32) * 0.1 + 0.001
        return {'x': x, 'gate_W_packed': gate_W_packed, 'gate_scales': gate_scales, 'up_W_packed': up_W_packed, 'up_scales': up_scales, 'down_W_packed': down_W_packed, 'down_scales': down_scales}
    _L0_ffn_in = _L0_ffn_setup()
    _d = {'L0_attn_x': _L0_attn_in['x'], 'L0_attn_W_Q': _L0_attn_in['W_Q'], 'L0_attn_W_K': _L0_attn_in['W_K'], 'L0_attn_W_V': _L0_attn_in['W_V'], 'L0_attn_W_O': _L0_attn_in['W_O'], 'L0_attn_b_Q': _L0_attn_in['b_Q'], 'L0_attn_b_K': _L0_attn_in['b_K'], 'L0_attn_b_V': _L0_attn_in['b_V'], 'L0_attn_b_O': _L0_attn_in['b_O'], 'L0_ffn_gate_W_packed': _L0_ffn_in['gate_W_packed'], 'L0_ffn_gate_scales': _L0_ffn_in['gate_scales'], 'L0_ffn_up_W_packed': _L0_ffn_in['up_W_packed'], 'L0_ffn_up_scales': _L0_ffn_in['up_scales'], 'L0_ffn_down_W_packed': _L0_ffn_in['down_W_packed'], 'L0_ffn_down_scales': _L0_ffn_in['down_scales']}
    _x0 = _d['L0_attn_x']
    _d['L0_attn_x'] = jax.random.normal(jax.random.fold_in(jax.random.key(seed), 1), (16, 256, 256), dtype=_x0.dtype)
    del _x0
    return _d

def reference(L0_attn_x, L0_attn_W_Q, L0_attn_W_K, L0_attn_W_V, L0_attn_W_O, L0_attn_b_Q, L0_attn_b_K, L0_attn_b_V, L0_attn_b_O, L0_ffn_gate_W_packed, L0_ffn_gate_scales, L0_ffn_up_W_packed, L0_ffn_up_scales, L0_ffn_down_W_packed, L0_ffn_down_scales):

    def _L0_attn_ref(x, W_Q, W_K, W_V, W_O, b_Q, b_K, b_V, b_O):
        import jax, jax.numpy as jnp
        import numpy as np
        BATCH, SEQ, D_MODEL, N_HEADS, D_HEAD = (2, 256, 256, 16, 128)
        ATTN_SCALE = np.sqrt(D_HEAD).astype(np.float32)
        IGNORE = jnp.float32(-100000.0)
        q = jnp.einsum('bpd,hde->bphe', x, W_Q) + b_Q
        k = jnp.einsum('bpd,hde->bphe', x, W_K) + b_K
        v = jnp.einsum('bpd,hde->bphe', x, W_V) + b_V
        scores = jnp.einsum('bqhe,bkhe->bhqk', q, k) / ATTN_SCALE
        S = x.shape[1]
        causal = jnp.tril(jnp.ones((S, S), bool))
        scores = jnp.where(causal, scores, IGNORE)
        attn = jax.nn.softmax(scores, axis=-1)
        z = jnp.einsum('bkhe,bhqk->bqhe', v, attn)
        out = jnp.einsum('bqhe,hed->bqd', z, W_O) + b_O
        return out

    def _L0_ffn_ref(x, gate_W_packed, gate_scales, up_W_packed, up_scales, down_W_packed, down_scales):
        import jax, jax.numpy as jnp
        import numpy as np
        BLOCK_SIZE = 32
        HIDDEN_SIZE = 256
        MLP_DIM = 2048
        NVFP4_LUT = jnp.array([0.0, 0.5, 1.0, 1.5, 2.0, 3.0, 4.0, 6.0, 0.0, -0.5, -1.0, -1.5, -2.0, -3.0, -4.0, -6.0], dtype=jnp.float32)

        def dequant_nvfp4(W_packed, scales, block=BLOCK_SIZE):
            N = W_packed.shape[0]
            low = W_packed & 15
            high = W_packed >> 4 & 15
            idx = jnp.stack([low, high], axis=-1).reshape(N, -1)
            vals = NVFP4_LUT[idx]
            K = vals.shape[1]
            vals = vals.reshape(N, K // block, block) * scales[:, :, None]
            return vals.reshape(N, K)
        B, S, H = x.shape
        xt = x.reshape(B * S, H)
        Wg = dequant_nvfp4(gate_W_packed, gate_scales)
        Wu = dequant_nvfp4(up_W_packed, up_scales)
        Wd = dequant_nvfp4(down_W_packed, down_scales)
        gate = jnp.einsum('th,nh->tn', xt, Wg)
        up = jnp.einsum('th,nh->tn', xt, Wu)
        gelu = jnp.tanh(0.7978845608028654 * (gate + 0.044715 * gate ** 3)) * gate * 0.5 + gate * 0.5
        inter = gelu * up
        out = jnp.einsum('tn,hn->th', inter, Wd)
        return out.reshape(B, S, H)
    x = L0_attn_x
    x = x + _layernorm(_L0_attn_ref(_layernorm(x, axis=-1), L0_attn_W_Q, L0_attn_W_K, L0_attn_W_V, L0_attn_W_O, L0_attn_b_Q, L0_attn_b_K, L0_attn_b_V, L0_attn_b_O), axis=-1)
    x = x + _layernorm(_L0_ffn_ref(_layernorm(x, axis=-1), L0_ffn_gate_W_packed, L0_ffn_gate_scales, L0_ffn_up_W_packed, L0_ffn_up_scales, L0_ffn_down_W_packed, L0_ffn_down_scales), axis=-1)
    return x

_drawn_inputs = setup_inputs


def setup_inputs(seed=0):
    import zlib

    import numpy as np

    out = dict(_drawn_inputs(seed))
    spreads = {'L0_attn_b_Q': (0.0, 0.1),
     'L0_attn_b_K': (0.0, 0.1),
     'L0_attn_b_V': (0.0, 0.1),
     'L0_attn_b_O': (0.0, 0.1)}
    factors = {}
    for name, (base, spread) in spreads.items():
        noise = np.random.default_rng([zlib.crc32(name.encode()), seed]).standard_normal(out[name].shape)
        drawn = base * np.exp(spread * noise) if base else spread * noise
        out[name] = jnp.asarray(drawn.astype(out[name].dtype))
    for name, factor in factors.items():
        out[name] = (out[name] * factor).astype(out[name].dtype)
    return out
```

```python
import concourse.bass as bass
from concourse import mybir
from contextlib import ExitStack

F32 = mybir.dt.float32
F32R = mybir.dt.float32r
I32 = mybir.dt.int32
F16 = mybir.dt.float16
ALU = mybir.AluOpType
ACT = mybir.ActivationFunctionType

P = 128
D = 256
KT = D // P
HEADS = 16
E = 128
SEQ = 256
CHUNK = 512
TT = CHUNK // P
TOKENS = 16 * SEQ
NCH = TOKENS // CHUNK
HG = 4
EPS = 1e-5
MASKED = -100000.0 * float(E) ** 0.5
SCALE = float(E) ** -0.5
MLP = 2048
NT = MLP // P
BLK = 32
GELU_C = 0.7978845608028654
GELU_A = 0.044715


class Tally:

    def __init__(self, sem, value=0):
        self.sem, self.value = sem, value

    def add(self, ins, by=1):
        ins.then_inc(self.sem, by)
        self.value += by
        return self.value


def attention_phase(nc, x_v, wq, wk, wv, wo, bq, bk, bv, bo, x1_v):
    with ExitStack() as ctx:
        def sb(name, shape, dt=F32):
            return ctx.enter_context(nc.sbuf_tensor(name, shape, dt))

        def sem(name):
            return ctx.enter_context(nc.semaphore(name))

        wq_p = [sb(f"wq_{s}", [P, HEADS, KT, E], F32R) for s in ("hi", "lo")]
        wk_p = [sb(f"wk_{s}", [P, HEADS, KT, E], F32R) for s in ("hi", "lo")]
        wv_p = [sb(f"wv_{s}", [P, HEADS, KT, E], F32R) for s in ("hi", "lo")]
        wo_p = [sb(f"wo_{s}", [P, HEADS, D], F32R) for s in ("hi", "lo")]
        RAW = 3
        raw = sb("w_raw", [P, RAW, 2, D])
        bias_q = sb("bias_q", [P, HEADS])
        bias_k = sb("bias_k", [P, HEADS])
        bias_v = sb("bias_v", [P, HEADS])
        bias_o = sb("bias_o", [P, D])
        mask = sb("mask", [P, SEQ])
        ident = sb("ident", [P, P])
        power = sb("power", [P, TT])
        x_in = sb("x_in", [P, TT, D])
        x_res = sb("x_res", [P, TT, D])
        xn = sb("xn", [P, TT, D])
        xnT = [sb(f"xnT_{s}", [P, KT, CHUNK], F32R) for s in ("hi", "lo")]
        qT = [[sb(f"qT{i}_{s}", [P, CHUNK], F32R) for s in ("hi", "lo")] for i in range(2)]
        kT = [[sb(f"kT{i}_{s}", [P, CHUNK], F32R) for s in ("hi", "lo")] for i in range(2)]
        v = [sb(f"v_{s}", [P, TT, HG * E], F32R) for s in ("hi", "lo")]
        probs = [[sb(f"probs{i}{b}", [P, 384]) for b in range(2)] for i in range(2)]
        pT = [[sb(f"pT{b}_{s}", [P, 384], F32R) for s in ("hi", "lo")] for b in range(2)]
        zT = [sb(f"zT_{s}", [P, CHUNK], F32R) for s in ("hi", "lo")]
        nmax = [[sb(f"nmax{i}{b}", [P, 2]) for b in range(2)] for i in range(2)]
        sums = [[sb(f"sums{i}{b}", [P, 2]) for b in range(2)] for i in range(2)]
        rsum = [sb(f"rsum{b}", [P, 2]) for b in range(2)]
        stats = sb("stats", [P, TT, 6])
        mv = sb("mv", [P, TT, 2])
        var_eps = sb("var_eps", [P, TT])
        rstd = sb("rstd", [P, TT])
        token = sb("token", [P, 2])

        FB, UB = 3, 3
        fbank = [ctx.enter_context(nc.psum_tensor(f"fbank{i}", [P, 512], F32)) for i in range(FB)]
        ubank = [ctx.enter_context(nc.psum_tensor(f"ubank{i}", [P, 512], F32)) for i in range(UB)]
        obank = [ctx.enter_context(nc.psum_tensor(f"obank{i}", [P, 2, D], F32)) for i in range(2)]

        s_w = [sem(f"w_loaded{i}") for i in range(RAW)]
        s_w_split = sem("w_split")
        s_bias = sem("bias_loaded")
        s_const = sem("const_ready")
        s_x = sem("x_loaded")
        s_xres = sem("x_res_loaded")
        s_res_used = sem("residual_added")
        s_stored = sem("x1_stored")
        s_var = sem("variance_ready")
        s_rstd = sem("rstd_ready")
        s_pool = sem("pool_chain")
        s_xn = sem("xn_ready")
        s_full = sem("full_ready")
        s_hi = sem("full_hi")
        s_lo = sem("full_lo")
        s_scores = sem("scores_ready")
        s_masked = sem("masked_ready")
        s_exp = sem("exp_ready")
        s_probs = sem("probs_ready")
        s_pT = sem("pT_ready")
        s_pT_hi = sem("pT_hi")
        s_pT_lo = sem("pT_lo")
        s_out = sem("out_ready")
        s_out_used = sem("out_evacuated")
        s_dve_held = sem("dve_held")
        s_pool_held = sem("pool_held")
        s_dve = sem("dve_chain")

        pairs = []
        for h in range(0, HEADS, HG):
            pairs += [((wq, wq_p, h), (wk, wk_p, h)), ((wv, wv_p, h), (wv, wv_p, h + 1)),
                      ((wv, wv_p, h + 2), (wv, wv_p, h + 3)),
                      ((wq, wq_p, h + 1), (wk, wk_p, h + 1)), ((wo, wo_p, h), (wo, wo_p, h + 1)),
                      ((wq, wq_p, h + 2), (wk, wk_p, h + 2)),
                      ((wq, wq_p, h + 3), (wk, wk_p, h + 3)),
                      ((wo, wo_p, h + 2), (wo, wo_p, h + 3))]

        def split_count(w, h):
            return 1 + [any(m[0] is w and m[2] == h for m in pair) for pair in pairs].index(True)

        FPC = 2 * HEADS + HEADS + (HEADS // HG) * TT + KT
        assert FPC % FB == 0
        UPC = 2 * HEADS
        FULL0 = KT + 2

        def step_plan(j):
            plan = []
            if j < HEADS - 1:
                plan += [("q", j + 1), ("k", j + 1), ("pT", j)]
                if j % HG == 0:
                    plan += [("v", t) for t in range(TT)]
                if j > 0:
                    plan += [("out", j - 1)]
                plan += [("scores", j + 1), ("z", j)]
            else:
                plan += [("xT", kt) for kt in range(KT)]
                plan += [("pT", j), ("out", j - 1), ("q", j + 1), ("k", j + 1), ("z", j),
                         ("scores", j + 1), ("out", j)]
            return plan

        FULLS = ("q", "k", "v", "z", "xT")
        order = [(j, what) for j in range(HEADS) for what in step_plan(j)]
        place = {}
        for j, what in order:
            if what[0] in FULLS:
                group = j // HG if what[0] == "v" else 0
                place[what + (group,)] = len(place)
        assert len(place) == FPC

        def full_index(kind, n, group=0):
            return place[(kind, n, group)]

        block = ctx.enter_context(nc.Block())

        @block.sync
        def _(sp):
            sp.dma_start(x_in[:], x_v[:, 0:TT, :]).then_inc(s_x, 16)
            for n, pair in enumerate(pairs):
                if n >= RAW:
                    sp.wait_ge(s_w_split, n - RAW + 1)
                for i, (w, _, h) in enumerate(pair):
                    if w is wo:
                        dst, src = raw[:, n % RAW, i, :], w[h, :, :]
                    else:
                        dst = raw[:, n % RAW, i, :].rearrange("p (k e) -> p k e", k=KT)
                        src = w[h, :, :].rearrange("(k p) e -> p k e", p=P)
                    sp.dma_start(dst, src).then_inc(s_w[n % RAW], 16)
                if n == RAW - 1:
                    sp.dma_start(bias_o[:], bo.partition_broadcast(P)).then_inc(s_bias, 16)
                    for dst, src in ((bias_q, bq), (bias_k, bk), (bias_v, bv)):
                        sp.dma_start(dst[:], src[:, :]).then_inc(s_bias, 16)
            sp.dma_start(x_res[:], x_v[:, 0:TT, :]).then_inc(s_xres, 16)

            def store(c):
                sp.wait_ge(s_res_used, c + 1)
                sp.dma_start(x1_v[:, bass.ds(c * TT, TT), :], xn[:]).then_inc(s_stored, 16)

            with sp.Fori(0, NCH - 1) as c:
                sp.wait_ge(s_xn, c + 1)
                sp.dma_start(x_in[:], x_v[:, bass.ds((c + 1) * TT, TT), :]).then_inc(s_x, 16)
                store(c)
                sp.dma_start(x_res[:], x_v[:, bass.ds((c + 1) * TT, TT), :]).then_inc(s_xres, 16)
            sp.wait_ge(s_xn, NCH)
            sp.dma_start(x_in[:], x_v[:, 0:TT, :]).then_inc(s_x, 16)
            store(NCH - 1)
            sp.wait_ge(s_stored, 16 + NCH * 16)

        @block.scalar
        def _(act):
            def split_hi(dst, bank, bias=None):
                if bias is None:
                    return act.activation(dst, bank, ACT.Copy)
                return act.activation(dst, bank, ACT.Identity, bias=bias)

            def full(n, dst, bank, bias=None):
                act.wait_ge(s_full, n + 1)
                split_hi(dst, bank, bias).then_inc(s_hi, 1)

            def exps(u, i, b):
                act.wait_ge(s_masked, u + 1)
                pr = probs[i][b]
                act.activation(pr[:, 0:P], pr[:, 0:P], ACT.Exp, bias=nmax[i][b][:, 0:1],
                               scale=-1.0, accum_out=sums[i][b][:, 0:1])
                act.activation(pr[:, P:384], pr[:, P:384], ACT.Exp, bias=nmax[i][b][:, 1:2],
                               scale=-1.0, accum_out=sums[i][b][:, 1:2]).then_inc(s_exp, 1)

            for kt in range(KT):
                full(kt, xnT[0][:, kt, :], fbank[kt % FB][:])
            act.wait_ge(s_bias, 64)
            full(KT, qT[0][0][:], fbank[KT % FB][:], bias_q[:, 0:1])
            full(KT + 1, kT[0][0][:], fbank[(KT + 1) % FB][:], bias_k[:, 0:1])
            for b in range(2):
                exps(b, 0, b)
            with act.Fori(0, NCH) as c:
                for j, what in order:
                    kind, m = what
                    if kind in FULLS:
                        i = full_index(kind, m, j // HG if kind == "v" else 0)
                        bank = fbank[(FULL0 + i) % FB][:]
                        n = c * FPC + (FULL0 + i)
                        h = m % HEADS
                        if kind == "q":
                            full(n, qT[h % 2][0][:], bank, bias_q[:, h:h + 1])
                        elif kind == "k":
                            full(n, kT[h % 2][0][:], bank, bias_k[:, h:h + 1])
                        elif kind == "v":
                            full(n, v[0][:, m, :], bank)
                        elif kind == "z":
                            full(n, zT[0][:], bank, bias_v[:, h:h + 1])
                        else:
                            full(n, xnT[0][:, m, :], bank)
                    elif kind == "pT":
                        for b in range(2):
                            u = 2 * m + b
                            act.wait_ge(s_pT, c * UPC + (u + 1))
                            split_hi(pT[b][0][:], ubank[u % UB][:, 0:384]).then_inc(s_pT_hi, 1)
                    elif kind == "scores":
                        for b in range(2):
                            exps(c * UPC + (2 * m + b), m % 2, b)

        @block.tensor
        def _(pe):
            def three(out, a, b, start, stop, skip=False):
                nc.tensor.matmul(out, a[0], b[0], start=start, stop=False, skip_group_check=skip)
                nc.tensor.matmul(out, a[0], b[1], start=False, stop=False, skip_group_check=skip)
                return nc.tensor.matmul(out, a[1], b[0], start=False, stop=stop,
                                        skip_group_check=skip)

            def bank_free(n):
                pe.wait_ge(s_lo, n - FB + 1)

            def project(n, bank, w, h, first):
                bank_free(n)
                for kt in range(KT):
                    last = three(bank, [p[:, h, kt, :] for p in w], [p[:, kt, :] for p in xnT],
                                 kt == 0, kt == KT - 1)
                last.then_inc(s_full, 1)

            def transpose_x(n, kt, bank):
                for t in range(TT):
                    last = nc.tensor.transpose(bank[:, t * P:(t + 1) * P],
                                               xn[:, t, kt * P:(kt + 1) * P], ident[:])
                last.then_inc(s_full, 1)

            def scores(i, b, bank):
                q, k = qT[i], kT[i]
                o = b * SEQ
                three(bank[:, 0:P], [p[:, o:o + P] for p in q], [p[:, o:o + P] for p in k],
                      True, True)
                three(bank[:, P:384], [p[:, o + P:o + SEQ] for p in q],
                      [p[:, o:o + SEQ] for p in k], True, True).then_inc(s_scores, 1)

            pe.wait_ge(s_const, 3)
            pe.wait_ge(s_xn, 1)
            for kt in range(KT):
                transpose_x(kt, kt, fbank[kt % FB])
            pe.wait_ge(s_lo, KT)
            pe.wait_ge(s_w_split, split_count(wk, 0))
            for m, w in ((0, wq_p), (1, wk_p)):
                n = KT + m
                if n >= FB:
                    bank_free(n)
                for kt in range(KT):
                    last = three(fbank[n % FB][:], [p[:, 0, kt, :] for p in w],
                                 [p[:, kt, :] for p in xnT], kt == 0, kt == KT - 1)
                last.then_inc(s_full, 1)
            pe.wait_ge(s_lo, KT + 2)
            for b in range(2):
                scores(0, b, ubank[b])

            with pe.Fori(0, NCH) as c:
                base = c * FPC
                for j, what in order:
                    kind, m = what
                    if kind in FULLS:
                        i = full_index(kind, m, j // HG if kind == "v" else 0)
                        bank = fbank[(FULL0 + i) % FB]
                        n = base + (FULL0 + i)
                    h = m % HEADS
                    if kind in ("q", "k"):
                        if kind == "q" and m < HEADS:
                            pe.wait_ge(s_w_split, split_count(wk, m))
                        if kind == "q" and m == HEADS:
                            pe.wait_ge(s_lo, base + (FULL0 + full_index("xT", KT - 1) + 1))
                        project(n, bank[:], wq_p if kind == "q" else wk_p, h, False)
                    elif kind == "xT":
                        bank_free(n)
                        if m == 0:
                            pe.wait_ge(s_xn, c + 2)
                        transpose_x(n, m, bank)
                    elif kind == "v":
                        if m == 0:
                            pe.wait_ge(s_w_split, split_count(wv, j + HG - 1))
                        bank_free(n)
                        for kt in range(KT):
                            last = three(bank[:].rearrange("p (h e) -> p h e", h=HG),
                                         [p[:, kt, m * P:(m + 1) * P] for p in xnT],
                                         [p[:, j:j + HG, kt, :] for p in wv_p],
                                         kt == 0, kt == KT - 1)
                        last.then_inc(s_full, 1)
                    elif kind == "scores":
                        pe.wait_ge(s_lo, base + (FULL0 + full_index("k", m) + 1))
                        for b in range(2):
                            u = 2 * m + b
                            if m == HEADS:
                                pe.wait_ge(s_pT_lo, c * UPC + (UPC - 1 + b))
                            elif u >= UB:
                                pe.wait_ge(s_pT_lo, c * UPC + (u - UB + 1))
                            scores(h % 2, b, ubank[(u % UPC) % UB])
                    elif kind == "pT":
                        for b in range(2):
                            u = 2 * m + b
                            bank = ubank[u % UB]
                            pr = probs[m % 2][b]
                            pe.wait_ge(s_probs, c * UPC + (u + 1))
                            nc.tensor.transpose(bank[:, 0:P], pr[:, 0:P], ident[:])
                            nc.tensor.transpose(bank[:, P:2 * P], pr[:, P:2 * P], ident[:])
                            nc.tensor.transpose(bank[:, 2 * P:384], pr[:, 2 * P:384],
                                                ident[:]).then_inc(s_pT, 1)
                    elif kind == "z":
                        bank_free(n)
                        if m % HG == 0:
                            pe.wait_ge(s_lo, base + (FULL0 + full_index("v", TT - 1, m // HG) + 1))
                        e0 = (m % HG) * E
                        for b in range(2):
                            pe.wait_ge(s_pT_lo, c * UPC + (2 * m + b + 1))
                            o = b * SEQ
                            three(bank[:, o:o + SEQ], [p[:, 2 * b, e0:e0 + E] for p in v],
                                  [p[:, 0:SEQ] for p in pT[b]], True, False)
                            last = three(bank[:, o + P:o + SEQ],
                                         [p[:, 2 * b + 1, e0:e0 + E] for p in v],
                                         [p[:, SEQ:384] for p in pT[b]], False, True)
                        last.then_inc(s_full, 1)
                    elif kind == "out":
                        pe.wait_ge(s_lo, base + (FULL0 + full_index("z", m) + 1))
                        if m == 0:
                            pe.wait_ge(s_out_used, c + 1)
                        pe.wait_ge(s_w_split, split_count(wo, m))
                        for t in range(TT):
                            last = three(obank[t // 2][:, t % 2, :],
                                         [p[:, t * P:(t + 1) * P] for p in zT],
                                         [p[:, m, :] for p in wo_p],
                                         m == 0 and t % 2 == 0, m == HEADS - 1, skip=True)
                        if m == HEADS - 1:
                            last.then_inc(s_out, 1)

        @block.vector
        def _(dve):
            chain = Tally(s_dve)

            def after(ins, loop=None):
                chain.add(ins)
                dve.wait_ge(s_dve, chain.value if loop is None else loop + chain.value)

            def full(n, dst, hi, bank, bias=None):
                dve.wait_ge(s_hi, n + 1)
                if bias is None:
                    ins = dve.tensor_tensor(dst, bank, hi.bitcast(F32), ALU.subtract)
                else:
                    ins = dve.scalar_tensor_tensor(dst, bank, bias, hi.bitcast(F32),
                                                   ALU.add, ALU.subtract)
                ins.then_inc(s_lo, 1)

            def mask_scores(u, i, b, bank):
                dve.wait_ge(s_scores, u + 1)
                dve.sem_inc(s_dve_held, 1)
                for lo, hi, part in ((0, P, 0), (P, 384, 1)):
                    last = dve.tensor_tensor_reduce(
                        out=probs[i][b][:, lo:hi], in0=bank[:, lo:hi],
                        in1=mask[:, SEQ - (hi - lo):SEQ], scale=-SCALE, scalar=3.0e38,
                        op0=ALU.add, op1=ALU.min, accum_out=nmax[i][b][:, part:part + 1])
                last.then_inc(s_masked, 1)

            def normalise(u, i, b, loop):
                dve.wait_ge(s_exp, u + 1)
                after(dve.reciprocal(rsum[b][:], sums[i][b][:]), loop)
                for lo, hi, part in ((0, P, 0), (P, 384, 1)):
                    last = dve.tensor_scalar_mul(probs[i][b][:, lo:hi], probs[i][b][:, lo:hi],
                                                 rsum[b][:, part:part + 1])
                last.then_inc(s_probs, 1)

            def moments(src, loop):
                for t in range(TT):
                    last = dve.bn_stats(stats[:, t, :], src[:, t, :])
                after(last, loop)
                dve.sem_inc(s_dve_held, 1)
                for t in range(TT):
                    last = dve.bn_aggr(mv[:, t, :], stats[:, t, :])
                last.then_inc(s_var, 1)

            def standardise(dst, src, count):
                dve.wait_ge(s_rstd, count)
                for t in range(TT):
                    last = dve.tensor_scalar(dst[:, t, :], src[:, t, :], mv[:, t, 0:1],
                                             rstd[:, t:t + 1], ALU.subtract, ALU.mult)
                return last

            dve.memset(token[:, 0:1], 0.0).then_inc(s_out_used, 1)
            dve.wait_ge(s_x, 16)
            moments(x_in, None)
            standardise(xn, x_in, 1).then_inc(s_xn, 1)
            for kt in range(KT):
                full(kt, xnT[1][:, kt, :], xnT[0][:, kt, :], fbank[kt % FB][:])
            dve.wait_ge(s_bias, 64)
            full(KT, qT[0][1][:], qT[0][0][:], fbank[KT % FB][:], bias_q[:, 0:1])
            full(KT + 1, kT[0][1][:], kT[0][0][:], fbank[(KT + 1) % FB][:], bias_k[:, 0:1])
            dve.wait_ge(s_const, 3)
            for b in range(2):
                mask_scores(b, 0, b, ubank[b])
            for b in range(2):
                normalise(b, 0, b, None)

            per_step = 2 * HEADS + 3
            start = chain.value
            with dve.Fori(0, NCH) as c:
                base = c * FPC
                loop = c * per_step
                for j, what in order:
                    kind, m = what
                    h = m % HEADS
                    if kind in FULLS:
                        i = full_index(kind, m, j // HG if kind == "v" else 0)
                        bank = fbank[(FULL0 + i) % FB][:]
                        n = base + (FULL0 + i)
                        if kind == "q":
                            full(n, qT[h % 2][1][:], qT[h % 2][0][:], bank, bias_q[:, h:h + 1])
                        elif kind == "k":
                            full(n, kT[h % 2][1][:], kT[h % 2][0][:], bank, bias_k[:, h:h + 1])
                        elif kind == "v":
                            full(n, v[1][:, m, :], v[0][:, m, :], bank)
                        elif kind == "z":
                            full(n, zT[1][:], zT[0][:], bank, bias_v[:, h:h + 1])
                            if j < HEADS - 1:
                                for b in range(2):
                                    normalise(c * UPC + (2 * (j + 1) + b), (j + 1) % 2, b, loop)
                            if j == HEADS - 4:
                                dve.wait_ge(s_x, c * 16 + 32)
                                dve.wait_ge(s_stored, c * 16 + 16)
                                moments(x_in, loop)
                                standardise(xn, x_in, c * 2 + 2).then_inc(s_xn, 1)
                        else:
                            full(n, xnT[1][:, m, :], xnT[0][:, m, :], bank)
                    elif kind == "pT":
                        for b in range(2):
                            u = 2 * m + b
                            dve.wait_ge(s_pT_hi, c * UPC + (u + 1))
                            dve.tensor_tensor(pT[b][1][:], ubank[u % UB][:, 0:384],
                                              pT[b][0][:].bitcast(F32),
                                              ALU.subtract).then_inc(s_pT_lo, 1)
                    elif kind == "scores":
                        for b in range(2):
                            u = 2 * m + b
                            mask_scores(c * UPC + u, h % 2, b, ubank[(u % UPC) % UB])
                        if m == HEADS:
                            for b in range(2):
                                normalise(c * UPC + (2 * m + b), h % 2, b, loop)
                dve.wait_ge(s_out, c + 1)
                for i in range(2):
                    last = dve.tensor_tensor(xn[:, 2 * i:2 * i + 2, :], obank[i][:],
                                             bias_o[:].unsqueeze(1).broadcast_to([P, 2, D]),
                                             ALU.add)
                last.then_inc(s_out_used, 1)
                dve.wait_ge(s_out_used, c + 2)
                moments(xn, loop)
                after(standardise(xn, xn, c * 2 + 3), loop)
                dve.wait_ge(s_xres, c * 16 + 16)
                dve.tensor_tensor(xn[:], xn[:], x_res[:], ALU.add).then_inc(s_res_used, 1)
            assert chain.value - start == per_step, (chain.value, start)

        @block.gpsimd
        def _(pool):
            pool.memset(ident[:], 0.0).then_inc(s_pool, 1)
            pool.memset(mask[:], 0.0).then_inc(s_pool, 1)
            pool.memset(power[:], -0.5).then_inc(s_const, 1)
            pool.memset(token[:, 1:2], 0.0).then_inc(s_stored, 16)
            pool.wait_ge(s_pool, 2)
            pool.affine_select(out=ident[:], in_=ident[:], compare_op=ALU.not_equal, fill=1.0,
                               base=0, pattern=[[-1, P]], channel_multiplier=1).then_inc(s_const, 1)
            pool.affine_select(out=mask[:, P:SEQ], in_=mask[:, P:SEQ], compare_op=ALU.is_ge,
                               fill=MASKED, base=0, pattern=[[-1, P]],
                               channel_multiplier=1).then_inc(s_const, 1)
            pool.wait_ge(s_const, 3)
            chain = Tally(s_pool, 2)

            def roots(count, loop):
                pool.wait_ge(s_var, count)
                pool.sem_inc(s_pool_held, 1)
                chain.add(pool.tensor_scalar(var_eps[:], mv[:, :, 1], EPS, 1.0, ALU.add, ALU.mult))
                pool.wait_ge(s_pool, chain.value if loop is None else loop + chain.value)
                pool.tensor_tensor(rstd[:], var_eps[:], power[:], ALU.pow).then_inc(s_rstd, 1)

            roots(1, None)
            for n, pair in enumerate(pairs):
                pool.wait_ge(s_w[n % RAW], 32 * (n // RAW + 1))
                views = []
                for i, (w, parts, h) in enumerate(pair):
                    src = raw[:, n % RAW, i, :]
                    if w is not wo:
                        src = src.rearrange("p (k e) -> p k e", k=KT)
                    views.append((src, parts[0][:, h], parts[1][:, h]))
                for src, hi, lo in views:
                    chain.add(pool.tensor_copy(hi, src))
                pool.wait_ge(s_pool, chain.value)
                for src, hi, lo in views:
                    last = pool.tensor_tensor(lo, src, hi.bitcast(F32), ALU.subtract)
                last.then_inc(s_w_split, 1)
            with pool.Fori(0, NCH) as c:
                roots(c * 2 + 2, c * 2)
                roots(c * 2 + 3, c * 2)


def mlp_phase(nc, x1_v, packed, scales, out_v):
    with ExitStack() as ctx:
        def sb(name, shape, dt=F32):
            return ctx.enter_context(nc.sbuf_tensor(name, shape, dt))

        def sem(name):
            return ctx.enter_context(nc.semaphore(name))

        wg_p = [sb(f"wg_{s}", [P, KT, MLP], F32R) for s in ("hi", "lo")]
        wu_p = [sb(f"wu_{s}", [P, KT, MLP], F32R) for s in ("hi", "lo")]
        wd_p = [sb(f"wd_{s}", [P, NT, D], F32R) for s in ("hi", "lo")]
        WORDS = MLP * D // 2 // P
        PW = 512
        words = [sb(f"words{i}", [P, PW], I32) for i in range(3)]
        scale = [sb(f"scale{i}", [P, PW]) for i in range(3)]
        spread = sb("spread", [P, PW], I32)
        signs = sb("signs", [P, PW], I32)
        codes = sb("codes", [P, PW], I32)
        wfull = [sb(f"wfull{i}", [P, 2, PW]) for i in range(2)]
        ident = sb("ident2", [P, P])
        power = sb("power2", [P, TT])
        x_in = sb("x1_in", [P, TT, D])
        x_res = sb("x1_res", [P, TT, D])
        xn = sb("x1n", [P, TT, D])
        y = sb("y", [P, TT, D])
        xnT = [sb(f"x1nT_{s}", [P, KT, CHUNK], F32R) for s in ("hi", "lo")]
        sq = [sb(f"sq{i}", [P, CHUNK]) for i in range(2)]
        th = [sb(f"th{i}", [P, CHUNK]) for i in range(2)]
        act_v = [sb(f"inter{i}", [P, CHUNK]) for i in range(2)]
        iT = [[sb(f"iT{i}_{s}", [P, CHUNK], F32R) for s in ("hi", "lo")] for i in range(4)]
        stats = sb("stats2", [P, TT, 6])
        mv = sb("mv2", [P, TT, 2])
        var_eps = sb("var_eps2", [P, TT])
        rstd = sb("rstd2", [P, TT])
        token = sb("token2", [P, 2])

        gbank = [ctx.enter_context(nc.psum_tensor(f"gbank{i}", [P, 512], F32)) for i in range(3)]
        hbank = [ctx.enter_context(nc.psum_tensor(f"hbank{i}", [P, 512], F32)) for i in range(3)]
        obank = [ctx.enter_context(nc.psum_tensor(f"dbank{i}", [P, 2, D], F32)) for i in range(2)]

        s_words = [sem(f"words_loaded{i}") for i in range(3)]
        s_const = sem("const2_ready")
        s_pool = sem("pool2_chain")
        s_dve = sem("dve2_chain")
        s_dve_held = sem("dve2_held")
        s_pool_held = sem("pool2_held")
        s_wfull = sem("weights_dequantised")
        s_w_hi = sem("weights_hi")
        s_w_lo = sem("weights_lo")
        s_x = sem("x1_loaded")
        s_xres = sem("x1_res_loaded")
        s_var = sem("variance2_ready")
        s_rstd = sem("rstd2_ready")
        s_xn = sem("x1n_ready")
        s_xT = sem("x1nT_ready")
        s_xT_hi = sem("x1nT_hi")
        s_xT_lo = sem("x1nT_lo")
        s_gu = sem("gate_up_ready")
        s_sq = sem("square_ready")
        s_arg = sem("tanh_argument_ready")
        s_tanh = sem("tanh_ready")
        s_inter = sem("inter_ready")
        s_iT_hi = sem("inter_hi")
        s_iT_lo = sem("inter_lo")
        s_down = sem("down_ready")
        s_down_used = sem("down_evacuated")
        s_y = sem("y_ready")
        s_stored = sem("out_stored")

        pieces = [(m, i) for i in range(WORDS // PW) for m in range(3)]

        def parts(n):
            m, i = pieces[n]
            if m < 2:
                return [[p[:, r, i * PW:(i + 1) * PW] for p in (wg_p, wu_p)[m]]
                        for r in range(2)]
            pairs = PW // D
            return [[p[:, 2 * pairs * i + r:2 * pairs * (i + 1):2, :] for p in wd_p]
                    for r in range(2)]

        def like(src, dst):
            return src if len(dst.shape) == 2 else src.rearrange("p (t h) -> p t h", h=D)

        def slot(j):
            return (j % NT) % 3

        def plan(j):
            if j == NT - 2:
                return [("xT", 0), ("down", j), ("gu", j + 2)]
            return [("gu", j + 2), ("down", j)]

        order = [(j, what) for j in range(NT) for what in plan(j)]
        block = ctx.enter_context(nc.Block())

        @block.sync
        def _(sp):
            sp.dma_start(x_in[:], x1_v[:, 0:TT, :]).then_inc(s_x, 16)
            for n, (m, i) in enumerate(pieces):
                if n >= 3:
                    sp.wait_ge(s_wfull, n - 2)
                sp.dma_start(words[n % 3][:],
                             packed[m][:, i * PW:(i + 1) * PW]).then_inc(s_words[n % 3], 16)
                for b in range(P // 16):
                    sp.dma_start(scale[n % 3][16 * b:16 * (b + 1), :],
                                 scales[m][b, i * PW:(i + 1) * PW].partition_broadcast(16)
                                 ).then_inc(s_words[n % 3], 16)
            sp.dma_start(x_res[:], x1_v[:, 0:TT, :]).then_inc(s_xres, 16)

            def store(c):
                sp.wait_ge(s_y, c + 1)
                sp.dma_start(out_v[:, bass.ds(c * TT, TT), :], y[:]).then_inc(s_stored, 16)

            with sp.Fori(0, NCH - 1) as c:
                sp.wait_ge(s_xn, c + 1)
                sp.dma_start(x_in[:], x1_v[:, bass.ds((c + 1) * TT, TT), :]).then_inc(s_x, 16)
                store(c)
                sp.dma_start(x_res[:], x1_v[:, bass.ds((c + 1) * TT, TT), :]).then_inc(s_xres, 16)
            sp.wait_ge(s_xn, NCH)
            sp.dma_start(x_in[:], x1_v[:, 0:TT, :]).then_inc(s_x, 16)
            store(NCH - 1)
            sp.wait_ge(s_stored, 16 + NCH * 16)

        @block.scalar
        def _(act):
            def x_hi(kt, count):
                act.wait_ge(s_xT, count)
                act.activation(xnT[0][:, kt, :], (gbank, hbank)[kt][2][:],
                               ACT.Copy).then_inc(s_xT_hi, 1)

            def square(n, j):
                act.wait_ge(s_gu, n + 1)
                act.activation(sq[j % 2][:], gbank[slot(j)][:], ACT.Square).then_inc(s_sq, 1)

            def tanh(n, j):
                act.wait_ge(s_arg, n + 1)
                act.activation(th[j % 2][:], th[j % 2][:], ACT.Tanh,
                               scale=GELU_C * GELU_A).then_inc(s_tanh, 1)

            def inter_hi(n, j):
                act.wait_ge(s_inter, n + 1)
                act.activation(iT[j % 4][0][:], act_v[j % 2][:], ACT.Copy).then_inc(s_iT_hi, 1)

            for n in range(len(pieces)):
                act.wait_ge(s_wfull, n + 1)
                for r, dst in enumerate(parts(n)):
                    last = act.activation(dst[0], like(wfull[n % 2][:, r, :], dst[0]), ACT.Copy)
                last.then_inc(s_w_hi, 1)
            for kt in range(KT):
                x_hi(kt, kt + 1)
            square(0, 0)
            tanh(0, 0)
            square(1, 1)
            inter_hi(0, 0)
            tanh(1, 1)
            with act.Fori(0, NCH) as c:
                base = c * NT
                for j, (kind, m) in order:
                    if kind == "xT":
                        for kt in range(KT):
                            x_hi(kt, c * KT + (KT + kt + 1))
                    elif kind == "gu":
                        square(base + m, m)
                        inter_hi(base + (m - 1), m - 1)
                        tanh(base + m, m)

        @block.tensor
        def _(pe):
            def three(out, a, b, start, stop, skip=False):
                nc.tensor.matmul(out, a[0], b[0], start=start, stop=False, skip_group_check=skip)
                nc.tensor.matmul(out, a[0], b[1], start=False, stop=False, skip_group_check=skip)
                return nc.tensor.matmul(out, a[1], b[0], start=False, stop=stop,
                                        skip_group_check=skip)

            def transpose_x(count):
                pe.wait_ge(s_xn, count)
                for kt in range(KT):
                    bank = (gbank, hbank)[kt][2]
                    for t in range(TT):
                        last = nc.tensor.transpose(bank[:, t * P:(t + 1) * P],
                                                   xn[:, t, kt:D:KT], ident[:])
                    last.then_inc(s_xT, 1)

            def gate_up(j):
                i = j % NT
                for w, banks in ((wg_p, gbank), (wu_p, hbank)):
                    for kt in range(KT):
                        last = three(banks[slot(j)][:], [p[:, kt, i * P:(i + 1) * P] for p in w],
                                     [p[:, kt, :] for p in xnT], kt == 0, kt == KT - 1)
                last.then_inc(s_gu, 1)

            pe.wait_ge(s_const, 2)
            transpose_x(1)
            pe.wait_ge(s_xT_lo, KT)
            pe.wait_ge(s_w_lo, len(pieces))
            gate_up(0)
            gate_up(1)
            with pe.Fori(0, NCH) as c:
                base = c * NT
                for j, (kind, m) in order:
                    if kind == "xT":
                        pe.wait_ge(s_inter, base + (m + NT - 1))
                        transpose_x(c + 2)
                    elif kind == "gu":
                        if m == NT:
                            pe.wait_ge(s_xT_lo, c * KT + 2 * KT)
                            pe.wait_ge(s_inter, base + NT)
                        elif 3 <= m < NT:
                            pe.wait_ge(s_inter, base + (m - 2))
                        gate_up(m)
                    else:
                        pe.wait_ge(s_iT_hi, base + (m + 1))
                        pe.wait_ge(s_iT_lo, base + (m + 1))
                        if m == 0:
                            pe.wait_ge(s_down_used, c + 1)
                        for t in range(TT):
                            last = three(obank[t // 2][:, t % 2, :],
                                         [p[:, t * P:(t + 1) * P] for p in iT[m % 4]],
                                         [p[:, m, :] for p in wd_p],
                                         m == 0 and t % 2 == 0, m == NT - 1, skip=True)
                        if m == NT - 1:
                            last.then_inc(s_down, 1)

        @block.vector
        def _(dve):
            chain = Tally(s_dve)

            def after(ins, loop=None):
                chain.add(ins)
                dve.wait_ge(s_dve, chain.value if loop is None else loop + chain.value)

            def moments(src, loop):
                for t in range(TT):
                    last = dve.bn_stats(stats[:, t, :], src(t))
                after(last, loop)
                dve.sem_inc(s_dve_held, 1)
                for t in range(TT):
                    last = dve.bn_aggr(mv[:, t, :], stats[:, t, :])
                last.then_inc(s_var, 1)

            def standardise(dst, src, count):
                dve.wait_ge(s_rstd, count)
                for t in range(TT):
                    last = dve.tensor_scalar(dst[:, t, :], src(t), mv[:, t, 0:1],
                                             rstd[:, t:t + 1], ALU.subtract, ALU.mult)
                return last

            def of_x(t):
                return x_in[:, t, :]

            def of_out(t):
                return obank[t // 2][:, t % 2, :]

            def x_lo(kt, count):
                dve.wait_ge(s_xT_hi, count)
                dve.tensor_tensor(xnT[1][:, kt, :], (gbank, hbank)[kt][2][:],
                                  xnT[0][:, kt, :].bitcast(F32), ALU.subtract).then_inc(s_xT_lo, 1)

            def argument(n, j):
                dve.wait_ge(s_sq, n + 1)
                dve.scalar_tensor_tensor(th[j % 2][:], sq[j % 2][:], 1.0 / GELU_A,
                                         gbank[slot(j)][:], ALU.add, ALU.mult).then_inc(s_arg, 1)

            def gated(n, j, loop):
                dve.wait_ge(s_tanh, n + 1)
                after(dve.scalar_tensor_tensor(act_v[j % 2][:], th[j % 2][:], 1.0,
                                               gbank[slot(j)][:], ALU.add, ALU.mult), loop)
                dve.scalar_tensor_tensor(act_v[j % 2][:], act_v[j % 2][:], 0.5,
                                         hbank[slot(j)][:], ALU.mult, ALU.mult).then_inc(s_inter, 1)

            dve.memset(token[:, 0:1], 0.0).then_inc(s_down_used, 1)

            def dequantise(n):
                w = words[n % 3][:]
                dve.wait_ge(s_words[n % 3], 16 * (1 + P // 16) * (n // 3 + 1))
                if n >= 2:
                    dve.wait_ge(s_w_lo, n - 1)
                after(dve.tensor_scalar(spread[:], w, 0xF0, 12, ALU.bitwise_and,
                                        ALU.logical_shift_left))
                after(dve.scalar_tensor_tensor(spread[:], w, 0xF, spread[:], ALU.bitwise_and,
                                               ALU.bitwise_or))
                dve.tensor_scalar(signs[:], spread[:], 0x80008, 12, ALU.bitwise_and,
                                  ALU.logical_shift_left)
                after(dve.tensor_scalar(codes[:], spread[:], 0x70007, 9, ALU.bitwise_and,
                                        ALU.logical_shift_left))
                after(dve.tensor_tensor(codes[:], codes[:], signs[:], ALU.bitwise_or))
                pair = codes[:].bitcast(F16).rearrange("p (w r) -> p r w", r=2)
                for r in range(2):
                    last = dve.scalar_tensor_tensor(wfull[n % 2][:, r, :], pair[:, r, :], 16384.0,
                                                    scale[n % 3][:], ALU.mult, ALU.mult)
                last.then_inc(s_wfull, 1)

            for n in range(len(pieces)):
                dequantise(n)
            dve.wait_ge(s_x, 16)
            moments(of_x, None)
            standardise(xn, of_x, 1).then_inc(s_xn, 1)
            for kt in range(KT):
                x_lo(kt, kt + 1)
            for j in range(2):
                argument(j, j)
                gated(j, j, None)
            per_step = NT + 2
            start = chain.value
            with dve.Fori(0, NCH) as c:
                base = c * NT
                loop = c * per_step
                for j, (kind, m) in order:
                    if kind == "xT":
                        for kt in range(KT):
                            x_lo(kt, c * KT + (KT + kt + 1))
                    elif kind == "gu":
                        if m >= 2:
                            argument(base + m, m)
                            dve.wait_ge(s_iT_lo, base + (m - 1))
                            gated(base + m, m, loop)
                        if m == NT - 4:
                            dve.wait_ge(s_x, c * 16 + 32)
                            moments(of_x, loop)
                            standardise(xn, of_x, c * 2 + 2).then_inc(s_xn, 1)
                dve.wait_ge(s_down, c + 1)
                moments(of_out, loop)
                dve.wait_ge(s_stored, c * 16 + 16)
                standardise(y, of_out, c * 2 + 3).then_inc(s_down_used, 1)
                dve.wait_ge(s_down_used, c + 2)
                dve.wait_ge(s_xres, c * 16 + 16)
                dve.tensor_tensor(y[:], y[:], x_res[:], ALU.add).then_inc(s_y, 1)
            assert chain.value - start == per_step

        @block.gpsimd
        def _(pool):
            pool.memset(power[:], -0.5).then_inc(s_pool, 1)
            pool.memset(ident[:], 0.0).then_inc(s_const, 1)
            pool.memset(token[:, 1:2], 0.0).then_inc(s_stored, 16)
            pool.wait_ge(s_const, 1)
            pool.affine_select(out=ident[:], in_=ident[:], compare_op=ALU.not_equal, fill=1.0,
                               base=0, pattern=[[-1, P]], channel_multiplier=1).then_inc(s_const, 1)
            chain = Tally(s_pool, 1)

            def roots(count, loop):
                pool.wait_ge(s_var, count)
                pool.sem_inc(s_pool_held, 1)
                chain.add(pool.tensor_scalar(var_eps[:], mv[:, :, 1], EPS, 1.0, ALU.add, ALU.mult))
                pool.wait_ge(s_pool, chain.value if loop is None else loop + chain.value)
                pool.tensor_tensor(rstd[:], var_eps[:], power[:], ALU.pow).then_inc(s_rstd, 1)

            def inter_lo(n, j):
                pool.wait_ge(s_iT_hi, n + 1)
                pool.tensor_tensor(iT[j % 4][1][:], act_v[j % 2][:], iT[j % 4][0][:].bitcast(F32),
                                   ALU.subtract).then_inc(s_iT_lo, 1)

            for n in range(len(pieces)):
                pool.wait_ge(s_w_hi, n + 1)
                for r, dst in enumerate(parts(n)):
                    last = pool.tensor_tensor(dst[1], like(wfull[n % 2][:, r, :], dst[1]),
                                              dst[0].bitcast(F32), ALU.subtract)
                last.then_inc(s_w_lo, 1)
            roots(1, None)
            inter_lo(0, 0)
            with pool.Fori(0, NCH) as c:
                base = c * NT
                for j, (kind, m) in order:
                    if kind == "gu":
                        inter_lo(base + (m - 1), m - 1)
                        if m == NT - 4:
                            roots(c * 2 + 2, c * 2)
                roots(c * 2 + 3, c * 2)


def block_kernel(nc, x, wq, wk, wv, wo, bq, bk, bv, bo, packed, scales, out):
    x_v = x.rearrange("b (t p) d -> p (b t) d", p=P)
    out_v = out.rearrange("b (t p) d -> p (b t) d", p=P)
    x1 = nc.dram_tensor("x1_scratch", (TOKENS, D), F32, kind="Internal").ap()
    x1_v = x1.rearrange("(t p) d -> p t d", p=P)
    attention_phase(nc, x_v, wq, wk, wv, wo, bq, bk, bv, bo, x1_v)
    mlp_phase(nc, x1_v, packed, scales, out_v)


_INS = ["L0_attn_x", "L0_attn_W_Q", "L0_attn_W_K", "L0_attn_W_V", "L0_attn_W_O",
        "L0_attn_b_Q", "L0_attn_b_K", "L0_attn_b_V", "L0_attn_b_O",
        "L0_ffn_gate_W_packed", "L0_ffn_gate_scales", "L0_ffn_up_W_packed", "L0_ffn_up_scales",
        "L0_ffn_down_W_packed", "L0_ffn_down_scales"]


def kernel(**inputs):
    import numpy as _np
    import concourse.bacc as _bacc
    from concourse import mybir as _mybir
    from concourse.bass_utils import run_bass_kernel_spmd as _run

    nc = _bacc.Bacc("TRN2", target_bir_lowering=False, num_devices=1)
    laid = {name: _np.asarray(inputs[name]) for name in _INS}
    for name in ("L0_attn_b_Q", "L0_attn_b_K", "L0_attn_b_V"):
        laid[name] = laid[name].T
    tiles = _np.arange(MLP).reshape(MLP // (2 * P), P, 2).transpose(0, 2, 1).reshape(MLP)
    for name in ("L0_ffn_gate_W_packed", "L0_ffn_gate_scales",
                 "L0_ffn_up_W_packed", "L0_ffn_up_scales"):
        laid[name] = laid[name][tiles].T
    for name in ("L0_ffn_down_W_packed", "L0_ffn_down_scales"):
        w = laid[name]
        groups = MLP // (2 * P)
        laid[name] = w.reshape(D, groups, -1).transpose(2, 1, 0).reshape(-1, groups * D)
    arrays, aps = {}, []
    for name in _INS:
        a = _np.ascontiguousarray(laid[name])
        arrays[f"in_{name}"] = a
        aps.append(nc.dram_tensor(f"in_{name}", a.shape, _mybir.dt.from_np(a.dtype),
                                  kind="ExternalInput").ap())
    out = nc.dram_tensor("out_0", (16, SEQ, D), _mybir.dt.float32, kind="ExternalOutput").ap()
    block_kernel(nc, *aps[:9], [aps[9], aps[11], aps[13]], [aps[10], aps[12], aps[14]], out)
    r = _run(nc, [arrays], core_ids=[0])
    return r.results[0]["out_0"]
```

```python
import concourse.bass as bass
from concourse import mybir
from contextlib import ExitStack

F32 = mybir.dt.float32
F32R = mybir.dt.float32r
I32 = mybir.dt.int32
F16 = mybir.dt.float16
ALU = mybir.AluOpType
ACT = mybir.ActivationFunctionType

P = 128
D = 256
KT = D // P
HEADS = 16
E = 128
SEQ = 256
CHUNK = 512
TT = CHUNK // P
TOKENS = 16 * SEQ
NCH = TOKENS // CHUNK
HG = 4
EPS = 1e-5
MASKED = -100000.0 * float(E) ** 0.5
SCALE = float(E) ** -0.5
MLP = 2048
NT = MLP // P
BLK = 32
PIECES = 3 * NT
PPS = PIECES // NCH
GELU_C = 0.7978845608028654
GELU_A = 0.044715


class Tally:

    def __init__(self, sem, value=0):
        self.sem, self.value = sem, value

    def add(self, ins, by=1):
        ins.then_inc(self.sem, by)
        self.value += by
        return self.value


PAIRS = [pair for h in range(0, HEADS, HG) for pair in (
    (("q", h), ("k", h)), (("v", h), ("v", h + 1)), (("v", h + 2), ("v", h + 3)),
    (("q", h + 1), ("k", h + 1)), (("o", h), ("o", h + 1)), (("q", h + 2), ("k", h + 2)),
    (("q", h + 3), ("k", h + 3)), (("o", h + 2), ("o", h + 3)))]


def attention_phase(nc, x_v, w_pairs, bq, bk, bv, bo, words_v, scales_v, x1_v, w4_v):
    with ExitStack() as ctx:
        def sb(name, shape, dt=F32):
            return ctx.enter_context(nc.sbuf_tensor(name, shape, dt))

        def sem(name):
            return ctx.enter_context(nc.semaphore(name))

        wqk_p = [sb(f"wqk_{s}", [P, HEADS, 2, KT, E], F32R) for s in ("hi", "lo")]
        wv_p = [sb(f"wv_{s}", [P, HEADS, KT, E], F32R) for s in ("hi", "lo")]
        wo_p = [sb(f"wo_{s}", [P, HEADS, D], F32R) for s in ("hi", "lo")]
        RAW = 2
        raw = sb("w_raw", [P, RAW, 2, D])
        bias_q = sb("bias_q", [P, HEADS])
        bias_k = sb("bias_k", [P, HEADS])
        bias_v = sb("bias_v", [P, HEADS])
        bias_o = sb("bias_o", [P, D])
        mask = sb("mask", [P, SEQ])
        ident = sb("ident", [P, P])
        power = sb("power", [P, TT])
        x_in = sb("x_in", [P, TT, D])
        x_res = sb("x_res", [P, TT, D])
        xn = sb("xn", [P, TT, D])
        xnT = [sb(f"xnT_{s}", [P, KT, CHUNK], F32R) for s in ("hi", "lo")]
        qT = [[sb(f"qT{i}_{s}", [P, CHUNK], F32R) for s in ("hi", "lo")] for i in range(2)]
        kT = [[sb(f"kT{i}_{s}", [P, CHUNK], F32R) for s in ("hi", "lo")] for i in range(2)]
        v = [sb(f"v_{s}", [P, TT, HG * E], F32R) for s in ("hi", "lo")]
        probs = [sb(f"probs{b}", [P, 384]) for b in range(2)]
        pT = [[sb(f"pT{b}_{s}", [P, 384], F32R) for s in ("hi", "lo")] for b in range(2)]
        zT = [sb(f"zT_{s}", [P, CHUNK], F32R) for s in ("hi", "lo")]
        words = sb("words", [P, P], I32)
        spread = sb("spread", [P, P], I32)
        scale = sb("scale", [P, P])
        w4 = sb("w4", [P, 2, P])
        w4_p = [[sb(f"w4_{i}{s}", [P, 2, P], F32R) for s in ("hi", "lo")] for i in range(2)]
        nmax = [[sb(f"nmax{i}{b}", [P, 2]) for b in range(2)] for i in range(2)]
        sums = [[sb(f"sums{i}{b}", [P, 2]) for b in range(2)] for i in range(2)]
        rsum = [[sb(f"rsum{i}{b}", [P, 2]) for b in range(2)] for i in range(2)]
        stats = sb("stats", [P, TT, 6])
        mv = sb("mv", [P, TT, 2])
        var_eps = sb("var_eps", [P, TT])
        rstd = sb("rstd", [P, TT])
        token = sb("token", [P, 2])

        FB, UB = 3, 3
        fbank = [ctx.enter_context(nc.psum_tensor(f"fbank{i}", [P, 512], F32)) for i in range(FB)]
        ubank = [ctx.enter_context(nc.psum_tensor(f"ubank{i}", [P, 512], F32)) for i in range(UB)]
        obank = [ctx.enter_context(nc.psum_tensor(f"obank{i}", [P, 2, D], F32)) for i in range(2)]

        s_w = [sem(f"w_loaded{i}") for i in range(RAW)]
        s_w_split = sem("w_split")
        s_bias = sem("bias_loaded")
        s_words = sem("words_loaded")
        s_w4 = sem("w4_dequantised")
        s_w4_hi = sem("w4_hi")
        s_w4_lo = sem("w4_lo")
        s_w4_stored = sem("w4_stored")
        s_const = sem("const_ready")
        s_x = sem("x_loaded")
        s_xres = sem("x_res_loaded")
        s_res_used = sem("residual_added")
        s_stored = sem("x1_stored")
        s_var = sem("variance_ready")
        s_rstd = sem("rstd_ready")
        s_pool = sem("pool_chain")
        s_xn = sem("xn_ready")
        s_full = sem("full_ready")
        s_hi = sem("full_hi")
        s_lo = sem("full_lo")
        s_scores = sem("scores_ready")
        s_masked = sem("masked_ready")
        s_exp = sem("exp_ready")
        s_rsum = sem("sums_inverted")
        s_probs = sem("probs_ready")
        s_pT = sem("pT_ready")
        s_pT_hi = sem("pT_hi")
        s_pT_lo = sem("pT_lo")
        s_out = sem("out_ready")
        s_out_used = sem("out_evacuated")
        s_dve_held = sem("dve_held")
        s_pool_held = sem("pool_held")
        s_dve = sem("dve_chain")

        def parts_of(pair):
            (kind, h), (other, _) = pair
            if kind == "q":
                return [p[:, h].rearrange("p m k e -> p m (k e)") for p in wqk_p]
            if kind == "v":
                return [p[:, h:h + 2].rearrange("p h k e -> p h (k e)") for p in wv_p]
            return [p[:, h:h + 2] for p in wo_p]

        def split_count(kind, h):
            return 1 + [(kind, h) in pair for pair in PAIRS].index(True)

        W4_SLOTS = [1, 3, 5, 7, 9, 11]
        X1_ROOTS, NEXT_ROOTS = 2, 10
        extras = {
            (0, "sum"): ("x1", 0), (0, "z"): ("x1", 1), (2, "sum"): ("x1", 2),
            (4, "sum"): ("x1", 3), (4, "z"): ("x1", 4), (6, "sum"): ("x1", 5), (6, "z"): ("x1", 6),
            (8, "sum"): ("next", 0), (8, "z"): ("next", 1), (10, "sum"): ("next", 2),
            (12, "sum"): ("next", 3), (12, "z"): ("next", 4),
        }
        for k, at in enumerate(W4_SLOTS):
            extras[at, "masked"] = ("spread0", k)
            extras[at, "sum"] = ("spread1", k)
            extras[at, "z"] = ("scaled", k)
        assert len(W4_SLOTS) == PPS

        FPC = 2 * HEADS + HEADS + (HEADS // HG) * TT + KT
        assert FPC % FB == 0
        UPC = 2 * HEADS
        FULL0 = KT + 2

        def step_plan(j):
            plan = [("q", j + 1), ("k", j + 1), ("pT", j)]
            if j == HEADS - 2:
                plan += [("xT", 0)]
            if j % HG == 0:
                plan += [("v", t) for t in range(TT)]
            if j > 0:
                plan += [("out", j - 1)]
            if j == HEADS - 2:
                plan += [("xT", 1)]
            if j < HEADS - 1:
                return plan + [("scores", j + 1), ("z", j)]
            return plan + [("z", j), ("scores", j + 1), ("out", j)]

        FULLS = ("q", "k", "v", "z", "xT")
        order = [(j, what) for j in range(HEADS) for what in step_plan(j)]
        place = {}
        for j, what in order:
            if what[0] in FULLS:
                group = j // HG if what[0] == "v" else 0
                place[what + (group,)] = len(place)
        assert len(place) == FPC

        def full_index(kind, n, group=0):
            return place[(kind, n, group)]

        block = ctx.enter_context(nc.Block())

        @block.sync
        def _(sp):
            sp.dma_start(x_in[:], x_v[:, 0:TT, :]).then_inc(s_x, 16)
            for n in range(len(PAIRS)):
                if n >= RAW:
                    sp.wait_ge(s_w_split, n - RAW + 1)
                sp.dma_start(raw[:, n % RAW], w_pairs[n]).then_inc(s_w[n % RAW], 16)
                if n == RAW - 1:
                    for dst, src in ((bias_q, bq), (bias_k, bk), (bias_v, bv)):
                        sp.dma_start(dst[:], src[:, :]).then_inc(s_bias, 16)
                    sp.dma_start(bias_o[:], bo.partition_broadcast(P)).then_inc(s_bias, 16)
                    sp.dma_start(x_res[:], x_v[:, 0:TT, :]).then_inc(s_xres, 16)

        @block.scalar
        def _(act):
            def split_hi(dst, bank, bias=None):
                if bias is None:
                    return act.activation(dst, bank, ACT.Copy)
                return act.activation(dst, bank, ACT.Identity, bias=bias)

            def full(n, dst, bank, bias=None):
                act.wait_ge(s_full, n + 1)
                split_hi(dst, bank, bias).then_inc(s_hi, 1)

            def exps(u, i, b):
                act.wait_ge(s_masked, u + 1)
                pr = probs[b]
                act.activation(pr[:, 0:P], pr[:, 0:P], ACT.Exp, bias=nmax[i][b][:, 0:1],
                               scale=-1.0, accum_out=sums[i][b][:, 0:1])
                act.activation(pr[:, P:384], pr[:, P:384], ACT.Exp, bias=nmax[i][b][:, 1:2],
                               scale=-1.0, accum_out=sums[i][b][:, 1:2]).then_inc(s_exp, 1)

            for kt in range(KT):
                full(kt, xnT[0][:, kt, :], fbank[kt % FB][:])
            act.wait_ge(s_bias, 64)
            full(KT, qT[0][0][:], fbank[KT % FB][:], bias_q[:, 0:1])
            full(KT + 1, kT[0][0][:], fbank[(KT + 1) % FB][:], bias_k[:, 0:1])
            for b in range(2):
                exps(b, 0, b)
            def finish(c):
                act.wait_ge(s_res_used, c * 2 + 2)
                act.dma_start(x1_v[:, bass.ds(c * TT, TT), :], xn[:]).then_inc(s_stored, 16)

            def w4_store(n, k):
                act.wait_ge(s_w4_lo, n + 2)
                for part in range(2):
                    act.dma_start(w4_v[part][:, bass.ds(n, 1)],
                                  w4_p[k % 2][part][:].bitcast(F32).unsqueeze(1)).then_inc(s_w4_stored, 16)

            def w4_hi(n, k):
                act.wait_ge(s_w4, n + 1)
                act.wait_ge(s_w4_stored, n * 32 + 32)
                act.activation(w4_p[k % 2][0][:], w4[:], ACT.Copy).then_inc(s_w4_hi, 1)

            def w4_load(n):
                act.dma_start(words[:], words_v[:, bass.ds(n * P, P)]).then_inc(s_words, 16)
                act.dma_start(scale[:], scales_v[:, bass.ds(n * P, P)].unsqueeze(1).broadcast_to(
                    [P // 16, 16, P])).then_inc(s_words, 16)

            w4_load(0)
            with act.Fori(0, NCH) as c:
                for j, what in order:
                    kind, m = what
                    if kind == "q" and j == 0:
                        act.wait_ge(s_xn, c + 1)
                        act.dma_start(x_in[:],
                                      x_v[:, bass.ds((c + 1) * TT, TT), :]).then_inc(s_x, 16)
                    if kind == "q" and j == 7:
                        finish(c)
                        act.dma_start(x_res[:],
                                      x_v[:, bass.ds(c * TT, TT), :]).then_inc(s_xres, 16)
                    if kind in FULLS:
                        i = full_index(kind, m, j // HG if kind == "v" else 0)
                        bank = fbank[(FULL0 + i) % FB][:]
                        n = c * FPC + (FULL0 + i)
                        h = m % HEADS
                        if kind == "q":
                            full(n, qT[h % 2][0][:], bank, bias_q[:, h:h + 1])
                        elif kind == "k":
                            full(n, kT[h % 2][0][:], bank, bias_k[:, h:h + 1])
                        elif kind == "v":
                            full(n, v[0][:, m, :], bank)
                        elif kind == "z":
                            full(n, zT[0][:], bank, bias_v[:, h:h + 1])
                        else:
                            full(n, xnT[0][:, m, :], bank)
                    elif kind == "pT":
                        for b in range(2):
                            u = 2 * m + b
                            act.wait_ge(s_pT, c * UPC + (u + 1))
                            split_hi(pT[b][0][:], ubank[u % UB][:, 0:384]).then_inc(s_pT_hi, 1)
                        for k, at in enumerate(W4_SLOTS):
                            if j == at + 2:
                                w4_store(c * PPS + k, k)
                        for k, at in enumerate(W4_SLOTS):
                            if j == at + 1:
                                w4_hi(c * PPS + k, k)
                                w4_load(c * PPS + (k + 1))
                    elif kind == "scores":
                        for b in range(2):
                            exps(c * UPC + (2 * m + b), m % 2, b)
            finish(NCH)
            act.wait_ge(s_stored, (NCH + 1) * 16)
            act.wait_ge(s_w4_stored, (PIECES + 2 - 1) * 32)
            act.wait_ge(s_words, (PIECES + 1) * 32)

        @block.tensor
        def _(pe):
            def three(out, a, b, start, stop, skip=False):
                nc.tensor.matmul(out, a[0], b[0], start=start, stop=False, skip_group_check=skip)
                nc.tensor.matmul(out, a[0], b[1], start=False, stop=False, skip_group_check=skip)
                return nc.tensor.matmul(out, a[1], b[0], start=False, stop=stop,
                                        skip_group_check=skip)

            def bank_free(n):
                pe.wait_ge(s_lo, n - FB + 1)

            def project(n, bank, h, which):
                bank_free(n)
                for kt in range(KT):
                    last = three(bank, [p[:, h, which, kt, :] for p in wqk_p],
                                 [p[:, kt, :] for p in xnT], kt == 0, kt == KT - 1)
                last.then_inc(s_full, 1)

            def transpose_x(n, kt, bank):
                for t in range(TT):
                    last = nc.tensor.transpose(bank[:, t * P:(t + 1) * P],
                                               xn[:, t, kt * P:(kt + 1) * P], ident[:])
                last.then_inc(s_full, 1)

            def scores(i, b, bank):
                q, k = qT[i], kT[i]
                o = b * SEQ
                three(bank[:, 0:P], [p[:, o:o + P] for p in q], [p[:, o:o + P] for p in k],
                      True, True)
                three(bank[:, P:384], [p[:, o + P:o + SEQ] for p in q],
                      [p[:, o:o + SEQ] for p in k], True, True).then_inc(s_scores, 1)

            pe.wait_ge(s_const, 3)
            pe.wait_ge(s_xn, 1)
            for kt in range(KT):
                transpose_x(kt, kt, fbank[kt % FB])
            pe.wait_ge(s_lo, KT)
            pe.wait_ge(s_w_split, split_count("k", 0))
            for m in range(2):
                n = KT + m
                if n >= FB:
                    bank_free(n)
                for kt in range(KT):
                    last = three(fbank[n % FB][:], [p[:, 0, m, kt, :] for p in wqk_p],
                                 [p[:, kt, :] for p in xnT], kt == 0, kt == KT - 1)
                last.then_inc(s_full, 1)
            pe.wait_ge(s_lo, KT + 2)
            for b in range(2):
                scores(0, b, ubank[b])

            with pe.Fori(0, NCH) as c:
                base = c * FPC
                for j, what in order:
                    kind, m = what
                    if kind in FULLS:
                        i = full_index(kind, m, j // HG if kind == "v" else 0)
                        bank = fbank[(FULL0 + i) % FB]
                        n = base + (FULL0 + i)
                    h = m % HEADS
                    if kind in ("q", "k"):
                        if kind == "q" and m < HEADS:
                            pe.wait_ge(s_w_split, split_count("k", m))
                        if kind == "q" and m == HEADS:
                            pe.wait_ge(s_lo, base + (FULL0 + full_index("xT", KT - 1) + 1))
                        project(n, bank[:], h, 0 if kind == "q" else 1)
                    elif kind == "xT":
                        bank_free(n)
                        if m == 0:
                            pe.wait_ge(s_xn, c + 2)
                        transpose_x(n, m, bank)
                    elif kind == "v":
                        if m == 0:
                            pe.wait_ge(s_w_split, split_count("v", j + HG - 1))
                        bank_free(n)
                        for kt in range(KT):
                            last = three(bank[:].rearrange("p (h e) -> p h e", h=HG),
                                         [p[:, kt, m * P:(m + 1) * P] for p in xnT],
                                         [p[:, j:j + HG, kt, :] for p in wv_p],
                                         kt == 0, kt == KT - 1)
                        last.then_inc(s_full, 1)
                    elif kind == "scores":
                        pe.wait_ge(s_lo, base + (FULL0 + full_index("k", m) + 1))
                        for b in range(2):
                            u = 2 * m + b
                            if m == HEADS:
                                pe.wait_ge(s_pT_lo, c * UPC + (UPC - 1 + b))
                            elif u >= UB:
                                pe.wait_ge(s_pT_lo, c * UPC + (u - UB + 1))
                            scores(h % 2, b, ubank[(u % UPC) % UB])
                    elif kind == "pT":
                        for b in range(2):
                            u = 2 * m + b
                            bank = ubank[u % UB]
                            pr = probs[b]
                            pe.wait_ge(s_probs, c * UPC + (u + 1))
                            nc.tensor.transpose(bank[:, 0:P], pr[:, 0:P], ident[:])
                            nc.tensor.transpose(bank[:, P:2 * P], pr[:, P:2 * P], ident[:])
                            nc.tensor.transpose(bank[:, 2 * P:384], pr[:, 2 * P:384],
                                                ident[:]).then_inc(s_pT, 1)
                    elif kind == "z":
                        bank_free(n)
                        if m % HG == 0:
                            pe.wait_ge(s_lo, base + (FULL0 + full_index("v", TT - 1, m // HG) + 1))
                        e0 = (m % HG) * E
                        for b in range(2):
                            pe.wait_ge(s_pT_lo, c * UPC + (2 * m + b + 1))
                            o = b * SEQ
                            three(bank[:, o:o + SEQ], [p[:, 2 * b, e0:e0 + E] for p in v],
                                  [p[:, 0:SEQ] for p in pT[b]], True, False)
                            last = three(bank[:, o + P:o + SEQ],
                                         [p[:, 2 * b + 1, e0:e0 + E] for p in v],
                                         [p[:, SEQ:384] for p in pT[b]], False, True)
                        last.then_inc(s_full, 1)
                    elif kind == "out":
                        pe.wait_ge(s_lo, base + (FULL0 + full_index("z", m) + 1))
                        if m == 0:
                            pe.wait_ge(s_out_used, c + 1)
                        pe.wait_ge(s_w_split, split_count("o", m))
                        for t in range(TT):
                            last = three(obank[t // 2][:, t % 2, :],
                                         [p[:, t * P:(t + 1) * P] for p in zT],
                                         [p[:, m, :] for p in wo_p],
                                         m == 0 and t % 2 == 0, m == HEADS - 1, skip=True)
                        if m == HEADS - 1:
                            last.then_inc(s_out, 1)

        @block.vector
        def _(dve):
            chain = Tally(s_dve)

            def after(ins, loop=None):
                chain.add(ins)
                dve.wait_ge(s_dve, chain.value if loop is None else loop + chain.value)

            def full(n, dst, hi, bank, bias=None):
                dve.wait_ge(s_hi, n + 1)
                if bias is None:
                    ins = dve.tensor_tensor(dst, bank, hi.bitcast(F32), ALU.subtract)
                else:
                    ins = dve.scalar_tensor_tensor(dst, bank, bias, hi.bitcast(F32),
                                                   ALU.add, ALU.subtract)
                ins.then_inc(s_lo, 1)

            def mask_scores(u, i, b, bank):
                dve.wait_ge(s_scores, u + 1)
                dve.sem_inc(s_dve_held, 1)
                for lo, hi, part in ((0, P, 0), (P, 384, 1)):
                    last = dve.tensor_tensor_reduce(
                        out=probs[b][:, lo:hi], in0=bank[:, lo:hi],
                        in1=mask[:, SEQ - (hi - lo):SEQ], scale=-SCALE, scalar=3.0e38,
                        op0=ALU.add, op1=ALU.min, accum_out=nmax[i][b][:, part:part + 1])
                last.then_inc(s_masked, 1)

            def invert_sums(u, i, b):
                dve.wait_ge(s_exp, u + 1)
                dve.reciprocal(rsum[i][b][:], sums[i][b][:]).then_inc(s_rsum, 1)

            def stats_of(src, t, loop):
                for i in (t, t + 1):
                    last = dve.bn_stats(stats[:, i, :], src[:, i, :])
                after(last, loop)

            def moments():
                dve.sem_inc(s_dve_held, 1)
                for t in range(TT):
                    last = dve.bn_aggr(mv[:, t, :], stats[:, t, :])
                last.then_inc(s_var, 1)

            def standardise(dst, src, t):
                for i in (t, t + 1):
                    last = dve.tensor_scalar(dst[:, i, :], src[:, i, :], mv[:, i, 0:1],
                                             rstd[:, i:i + 1], ALU.subtract, ALU.mult)
                return last

            def finish_x1(part, c, loop):
                if part in (0, 1):
                    stats_of(xn, 2 * part, loop)
                elif part == 2:
                    moments()
                elif part in (3, 4):
                    dve.wait_ge(s_rstd, c * 2 + 2)
                    after(standardise(xn, xn, 2 * (part - 3)), loop)
                else:
                    t = 2 * (part - 5)
                    dve.wait_ge(s_xres, c * 16 + 16)
                    dve.tensor_tensor(xn[:, t:t + 2, :], xn[:, t:t + 2, :], x_res[:, t:t + 2, :],
                                      ALU.add).then_inc(s_res_used, 1)

            def norm_next_x(part, c, loop):
                if part in (0, 1):
                    dve.wait_ge(s_x, c * 16 + 32)
                    stats_of(x_in, 2 * part, loop)
                elif part == 2:
                    moments()
                elif part in (3, 4):
                    dve.wait_ge(s_rstd, c * 2 + 3)
                    dve.wait_ge(s_stored, c * 16 + 16)
                    last = standardise(xn, x_in, 2 * (part - 3))
                    if part == 4:
                        last.then_inc(s_xn, 1)

            def spread0(n, loop):
                dve.wait_ge(s_words, n * 32 + 32)
                after(dve.tensor_scalar(spread[:], words[:], 0xF0, 12, ALU.bitwise_and,
                                        ALU.logical_shift_left), loop)
                after(dve.scalar_tensor_tensor(spread[:], words[:], 0xF, spread[:],
                                               ALU.bitwise_and, ALU.bitwise_or), loop)

            def spread1(loop):
                dve.tensor_scalar(words[:], spread[:], 0x80008, 12, ALU.bitwise_and,
                                  ALU.logical_shift_left)
                after(dve.tensor_scalar(spread[:], spread[:], 0x70007, 9, ALU.bitwise_and,
                                        ALU.logical_shift_left), loop)
                after(dve.tensor_tensor(spread[:], spread[:], words[:], ALU.bitwise_or), loop)

            def scaled(n):
                dve.wait_ge(s_w4_lo, n + 1)
                pair = spread[:].bitcast(F16).rearrange("p (w r) -> p r w", r=2)
                for r in range(2):
                    last = dve.scalar_tensor_tensor(w4[:, r, :], pair[:, r, :], 16384.0,
                                                    scale[:], ALU.mult, ALU.mult)
                last.then_inc(s_w4, 1)

            def extra(j, place, c, loop):
                work, part = extras.get((j, place), (None, 0))
                if work == "x1":
                    finish_x1(part, c, loop)
                elif work == "next":
                    norm_next_x(part, c, loop)
                elif work == "spread0":
                    spread0(c * PPS + part, loop)
                elif work == "spread1":
                    spread1(loop)
                elif work == "scaled":
                    scaled(c * PPS + part)

            dve.memset(token[:, 0:1], 0.0).then_inc(s_out_used, 1)
            dve.wait_ge(s_x, 16)
            for t in (0, 2):
                stats_of(x_in, t, None)
            moments()
            dve.wait_ge(s_rstd, 1)
            for t in (0, 2):
                last = standardise(xn, x_in, t)
            last.then_inc(s_xn, 1)
            for kt in range(KT):
                full(kt, xnT[1][:, kt, :], xnT[0][:, kt, :], fbank[kt % FB][:])
            dve.wait_ge(s_bias, 64)
            full(KT, qT[0][1][:], qT[0][0][:], fbank[KT % FB][:], bias_q[:, 0:1])
            full(KT + 1, kT[0][1][:], kT[0][0][:], fbank[(KT + 1) % FB][:], bias_k[:, 0:1])
            dve.wait_ge(s_const, 3)
            for b in range(2):
                mask_scores(b, 0, b, ubank[b])
            for b in range(2):
                invert_sums(b, 0, b)

            per_step = 6 + 4 * PPS
            start = chain.value
            with dve.Fori(0, NCH) as c:
                base = c * FPC
                loop = c * per_step
                for j, what in order:
                    kind, m = what
                    h = m % HEADS
                    if kind in FULLS:
                        i = full_index(kind, m, j // HG if kind == "v" else 0)
                        bank = fbank[(FULL0 + i) % FB][:]
                        n = base + (FULL0 + i)
                        if kind == "q":
                            full(n, qT[h % 2][1][:], qT[h % 2][0][:], bank, bias_q[:, h:h + 1])
                        elif kind == "k":
                            full(n, kT[h % 2][1][:], kT[h % 2][0][:], bank, bias_k[:, h:h + 1])
                        elif kind == "v":
                            full(n, v[1][:, m, :], v[0][:, m, :], bank)
                        elif kind == "z":
                            full(n, zT[1][:], zT[0][:], bank, bias_v[:, h:h + 1])
                            extra(j, "z", c, loop)
                        else:
                            full(n, xnT[1][:, m, :], xnT[0][:, m, :], bank)
                    elif kind == "pT":
                        for b in range(2):
                            u = 2 * m + b
                            dve.wait_ge(s_pT_hi, c * UPC + (u + 1))
                            dve.tensor_tensor(pT[b][1][:], ubank[u % UB][:, 0:384],
                                              pT[b][0][:].bitcast(F32),
                                              ALU.subtract).then_inc(s_pT_lo, 1)
                    elif kind == "scores":
                        for b in range(2):
                            u = 2 * m + b
                            mask_scores(c * UPC + u, h % 2, b, ubank[(u % UPC) % UB])
                        extra(j, "masked", c, loop)
                        for b in range(2):
                            invert_sums(c * UPC + (2 * m + b), h % 2, b)
                            if b == 0:
                                extra(j, "sum", c, loop)
                dve.wait_ge(s_out, c + 1)
                for i in range(2):
                    last = dve.tensor_tensor(xn[:, 2 * i:2 * i + 2, :], obank[i][:],
                                             bias_o[:].unsqueeze(1).broadcast_to([P, 2, D]),
                                             ALU.add)
                last.then_inc(s_out_used, 1)
                dve.wait_ge(s_out_used, c + 2)
            assert chain.value - start == per_step, (chain.value, start)
            for part in range(7):
                finish_x1(part, NCH, NCH * per_step - per_step)

        @block.gpsimd
        def _(pool):
            pool.memset(ident[:], 0.0).then_inc(s_pool, 1)
            pool.memset(mask[:], 0.0).then_inc(s_pool, 1)
            pool.memset(power[:], -0.5).then_inc(s_const, 1)
            pool.wait_ge(s_pool, 2)
            pool.affine_select(out=ident[:], in_=ident[:], compare_op=ALU.not_equal, fill=1.0,
                               base=0, pattern=[[-1, P]], channel_multiplier=1).then_inc(s_const, 1)
            pool.affine_select(out=mask[:, P:SEQ], in_=mask[:, P:SEQ], compare_op=ALU.is_ge,
                               fill=MASKED, base=0, pattern=[[-1, P]],
                               channel_multiplier=1).then_inc(s_const, 1)
            pool.wait_ge(s_const, 3)
            chain = Tally(s_pool, 2)

            def roots(count, loop):
                pool.wait_ge(s_var, count)
                pool.sem_inc(s_pool_held, 1)
                chain.add(pool.tensor_scalar(var_eps[:], mv[:, :, 1], EPS, 1.0, ALU.add, ALU.mult))
                pool.wait_ge(s_pool, chain.value if loop is None else loop + chain.value)
                pool.tensor_tensor(rstd[:], var_eps[:], power[:], ALU.pow).then_inc(s_rstd, 1)

            roots(1, None)
            def w4_lo(n, k):
                pool.wait_ge(s_w4_hi, n + 1)
                pool.tensor_tensor(w4_p[k % 2][1][:], w4[:], w4_p[k % 2][0][:].bitcast(F32),
                                   ALU.subtract).then_inc(s_w4_lo, 1)

            def normalise(u, i, b):
                pool.wait_ge(s_rsum, u + 1)
                pool.sem_inc(s_pool_held, 1)
                for lo, hi, part in ((0, P, 0), (P, 384, 1)):
                    last = pool.tensor_scalar(probs[b][:, lo:hi], probs[b][:, lo:hi],
                                              rsum[i][b][:, part:part + 1], 1.0,
                                              ALU.mult, ALU.mult)
                last.then_inc(s_probs, 1)

            def slot(c, j, loop):
                if j - 1 in W4_SLOTS:
                    w4_lo(c * PPS + W4_SLOTS.index(j - 1), W4_SLOTS.index(j - 1))
                for b in range(2):
                    normalise(c * UPC + (2 * (j + 1) + b), (j + 1) % 2, b)
                if j == X1_ROOTS:
                    roots(c * 2 + 2, loop)
                if j == NEXT_ROOTS:
                    roots(c * 2 + 3, loop)

            pool.memset(token[:, 0:1], 0.0).then_inc(s_w4_lo, 1)
            pool.memset(token[:, 1:2], 0.0).then_inc(s_w4_stored, 32)

            done = 0
            for n, pair in enumerate(PAIRS):
                pool.wait_ge(s_w[n % RAW], 16 * (n // RAW + 1))
                hi, lo = parts_of(pair)
                chain.add(pool.tensor_scalar(hi, raw[:, n % RAW], 1.0, 1.0, ALU.mult, ALU.mult))
                pool.wait_ge(s_pool, chain.value)
                last = pool.tensor_tensor(lo, raw[:, n % RAW], hi.bitcast(F32), ALU.subtract)
                last.then_inc(s_w_split, 1)
                if n == 4:
                    for b in range(2):
                        normalise(b, 0, b)
                if n >= 8 and n % 2 == 0:
                    slot(0, done, None)
                    done += 1
            for j in range(done, HEADS):
                slot(0, j, None)
            with pool.Fori(1, NCH) as c:
                for j in range(HEADS):
                    slot(c, j, (c - 1) * 2)
            roots(NCH * 2 + 2, (NCH - 2) * 2)


def mlp_phase(nc, x1_v, w4_v, out_v):
    with ExitStack() as ctx:
        def sb(name, shape, dt=F32):
            return ctx.enter_context(nc.sbuf_tensor(name, shape, dt))

        def sem(name):
            return ctx.enter_context(nc.semaphore(name))

        w4 = [sb(f"w4all_{s}", [P, PIECES, 2, P], F32R) for s in ("hi", "lo")]
        ident = sb("ident2", [P, P])
        power = sb("power2", [P, TT])
        x_in = sb("x1_in", [P, TT, D])
        x_res = sb("x1_res", [P, TT, D])
        xn = sb("x1n", [P, TT, D])
        y = sb("y", [P, TT, D])
        xnT = [sb(f"x1nT_{s}", [P, KT, CHUNK], F32R) for s in ("hi", "lo")]
        sq = [sb(f"sq{i}", [P, CHUNK]) for i in range(2)]
        th = [sb(f"th{i}", [P, CHUNK]) for i in range(2)]
        act_v = [sb(f"inter{i}", [P, CHUNK]) for i in range(2)]
        iT = [[sb(f"iT{i}_{s}", [P, CHUNK], F32R) for s in ("hi", "lo")] for i in range(4)]
        stats = sb("stats2", [P, TT, 6])
        mv = sb("mv2", [P, TT, 2])
        var_eps = sb("var_eps2", [P, TT])
        rstd = sb("rstd2", [P, TT])
        token = sb("token2", [P, 2])

        gbank = [ctx.enter_context(nc.psum_tensor(f"gbank{i}", [P, 512], F32)) for i in range(3)]
        hbank = [ctx.enter_context(nc.psum_tensor(f"hbank{i}", [P, 512], F32)) for i in range(3)]
        obank = [ctx.enter_context(nc.psum_tensor(f"dbank{i}", [P, 2, D], F32)) for i in range(2)]

        s_w4 = [sem(f"w4_loaded{q}") for q in range(NT // 2)]
        s_const = sem("const2_ready")
        s_pool = sem("pool2_chain")
        s_dve = sem("dve2_chain")
        s_dve_held = sem("dve2_held")
        s_pool_held = sem("pool2_held")
        s_x = sem("x1_loaded")
        s_xres = sem("x1_res_loaded")
        s_var = sem("variance2_ready")
        s_rstd = sem("rstd2_ready")
        s_xn = sem("x1n_ready")
        s_xT = sem("x1nT_ready")
        s_xT_hi = sem("x1nT_hi")
        s_xT_lo = sem("x1nT_lo")
        s_gu = sem("gate_up_ready")
        s_sq = sem("square_ready")
        s_arg = sem("tanh_argument_ready")
        s_tanh = sem("tanh_ready")
        s_inter = sem("inter_ready")
        s_iT_hi = sem("inter_hi")
        s_iT_lo = sem("inter_lo")
        s_down = sem("down_ready")
        s_down_used = sem("down_evacuated")
        s_y = sem("y_ready")
        s_stored = sem("out_stored")

        def slot(j):
            return (j % NT) % 3

        def plan(j):
            if j == NT - 3:
                return [("gu", j + 2), ("xT", 0), ("down", j)]
            if j == NT - 2:
                return [("down", j), ("gu", j + 2)]
            return [("gu", j + 2), ("down", j)]

        order = [(j, what) for j in range(NT) for what in plan(j)]
        block = ctx.enter_context(nc.Block())

        @block.sync
        def _(sp):
            sp.dma_start(x_in[:], x1_v[:, 0:TT, :]).then_inc(s_x, 16)
            for q in range(NT // 2):
                for part in range(2):
                    sp.dma_start(w4[part][:, q * 6:q * 6 + 6].bitcast(F32), w4_v[part][:, q * 6:q * 6 + 6]
                                 ).then_inc(s_w4[q], 16)
            sp.dma_start(x_res[:], x1_v[:, 0:TT, :]).then_inc(s_xres, 16)

            def look_ahead(c):
                sp.wait_ge(s_xn, c + 1)
                if c is NCH - 1:
                    sp.dma_start(x_in[:], x1_v[:, 0:TT, :]).then_inc(s_x, 16)
                else:
                    sp.dma_start(x_in[:], x1_v[:, bass.ds((c + 1) * TT, TT), :]).then_inc(s_x, 16)

            def finish(c):
                sp.wait_ge(s_y, c + 1)
                sp.dma_start(out_v[:, bass.ds((c - 1) * TT, TT), :], y[:]).then_inc(s_stored, 16)

            def residual(c):
                sp.dma_start(x_res[:], x1_v[:, bass.ds(c * TT, TT), :]).then_inc(s_xres, 16)

            look_ahead(0)
            sp.wait_ge(s_y, 1)
            residual(0)
            with sp.Fori(1, NCH - 1) as c:
                look_ahead(c)
                finish(c)
                residual(c)
            look_ahead(NCH - 1)
            finish(NCH - 1)
            residual(NCH - 1)
            finish(NCH)
            sp.wait_ge(s_stored, 16 + NCH * 16)

        @block.scalar
        def _(act):
            def x_hi(kt, count):
                act.wait_ge(s_xT, count)
                act.activation(xnT[0][:, kt, :], (gbank, hbank)[kt][2][:],
                               ACT.Copy).then_inc(s_xT_hi, 1)

            def square(n, j):
                act.wait_ge(s_gu, n + 1)
                act.activation(sq[j % 2][:], gbank[slot(j)][:], ACT.Square).then_inc(s_sq, 1)

            def tanh(n, j):
                act.wait_ge(s_arg, n + 1)
                act.activation(th[j % 2][:], th[j % 2][:], ACT.Tanh,
                               scale=GELU_C * GELU_A).then_inc(s_tanh, 1)

            def inter_hi(n, j):
                act.wait_ge(s_inter, n + 1)
                act.activation(iT[j % 4][0][:], act_v[j % 2][:], ACT.Copy).then_inc(s_iT_hi, 1)

            for kt in range(KT):
                x_hi(kt, kt + 1)
            square(0, 0)
            tanh(0, 0)
            square(1, 1)
            inter_hi(0, 0)
            tanh(1, 1)
            with act.Fori(0, NCH) as c:
                base = c * NT
                for j, (kind, m) in order:
                    if kind == "xT":
                        for kt in range(KT):
                            x_hi(kt, c * KT + (KT + kt + 1))
                    elif kind == "gu":
                        square(base + m, m)
                        inter_hi(base + (m - 1), m - 1)
                        tanh(base + m, m)
                act.wait_ge(s_stored, c * 16 + 16)
                act.wait_ge(s_down, c + 1)
                for i in range(2):
                    last = act.activation(y[:, 2 * i:2 * i + 2, :], obank[i][:], ACT.Copy)
                last.then_inc(s_down_used, 1)

        @block.tensor
        def _(pe):
            def three(out, a, b, start, stop, skip=False):
                nc.tensor.matmul(out, a[0], b[0], start=start, stop=False, skip_group_check=skip)
                nc.tensor.matmul(out, a[0], b[1], start=False, stop=False, skip_group_check=skip)
                return nc.tensor.matmul(out, a[1], b[0], start=False, stop=stop,
                                        skip_group_check=skip)

            def transpose_x(count):
                pe.wait_ge(s_xn, count)
                for kt in range(KT):
                    bank = (gbank, hbank)[kt][2]
                    for t in range(TT):
                        last = nc.tensor.transpose(bank[:, t * P:(t + 1) * P],
                                                   xn[:, t, kt:D:KT], ident[:])
                    last.then_inc(s_xT, 1)

            def gate_up(j):
                i = j % NT
                if i % 2 == 0:
                    pe.wait_ge(s_w4[i // 2], 32)
                for up, banks in ((0, gbank), (1, hbank)):
                    for kt in range(KT):
                        n = 6 * (i // 2) + 2 * (i % 2) + up
                        last = three(banks[slot(j)][:], [p[:, n, kt, :] for p in w4],
                                     [p[:, kt, :] for p in xnT], kt == 0, kt == KT - 1)
                last.then_inc(s_gu, 1)

            pe.wait_ge(s_const, 2)
            transpose_x(1)
            pe.wait_ge(s_xT_lo, KT)
            gate_up(0)
            gate_up(1)
            with pe.Fori(0, NCH) as c:
                base = c * NT
                for j, (kind, m) in order:
                    if kind == "xT":
                        pe.wait_ge(s_inter, base + (NT - 1))
                        transpose_x(c + 2)
                    elif kind == "gu":
                        if m == NT:
                            pe.wait_ge(s_xT_lo, c * KT + 2 * KT)
                            pe.wait_ge(s_inter, base + NT)
                        elif 3 <= m < NT:
                            pe.wait_ge(s_inter, base + (m - 2))
                        gate_up(m)
                    else:
                        pe.wait_ge(s_iT_hi, base + (m + 1))
                        pe.wait_ge(s_iT_lo, base + (m + 1))
                        if m == 0:
                            pe.wait_ge(s_down_used, c + 1)
                        for t in range(TT):
                            out = obank[t // 2][:, t % 2, :].rearrange("p (h e) -> p h e", e=P)
                            n = 6 * (m // 2) + 4
                            last = three(out, [p[:, t * P:(t + 1) * P] for p in iT[m % 4]],
                                         [p[:, n:n + 2, m % 2, :] for p in w4],
                                         m == 0 and t % 2 == 0, m == NT - 1, skip=True)
                        if m == NT - 1:
                            last.then_inc(s_down, 1)

        @block.vector
        def _(dve):
            chain = Tally(s_dve)

            def after(ins, loop=None):
                chain.add(ins)
                dve.wait_ge(s_dve, chain.value if loop is None else loop + chain.value)

            def stats_of(src, t, loop):
                for i in (t, t + 1):
                    last = dve.bn_stats(stats[:, i, :], src[:, i, :])
                after(last, loop)

            def moments():
                dve.sem_inc(s_dve_held, 1)
                for t in range(TT):
                    last = dve.bn_aggr(mv[:, t, :], stats[:, t, :])
                last.then_inc(s_var, 1)

            def standardise(dst, src, t):
                for i in (t, t + 1):
                    last = dve.tensor_scalar(dst[:, i, :], src[:, i, :], mv[:, i, 0:1],
                                             rstd[:, i:i + 1], ALU.subtract, ALU.mult)
                return last

            def finish_y(part, c, loop):
                if part in (0, 1):
                    dve.wait_ge(s_down_used, c + 1)
                    stats_of(y, 2 * part, loop)
                    if part == 1:
                        moments()
                elif part in (2, 3):
                    dve.wait_ge(s_rstd, c * 2 + 2)
                    after(standardise(y, y, 2 * (part - 2)), loop)
                else:
                    t = 2 * (part - 4)
                    dve.wait_ge(s_xres, c * 16 + 16)
                    last = dve.tensor_tensor(y[:, t:t + 2, :], y[:, t:t + 2, :],
                                             x_res[:, t:t + 2, :], ALU.add)
                    if part == 5:
                        last.then_inc(s_y, 1)

            def norm_next_x(part, c, loop):
                if part in (0, 1):
                    dve.wait_ge(s_x, c * 16 + 32)
                    stats_of(x_in, 2 * part, loop)
                    if part == 1:
                        moments()
                elif part in (2, 3):
                    dve.wait_ge(s_rstd, c * 2 + 3)
                    last = standardise(xn, x_in, 2 * (part - 2))
                    if part == 3:
                        last.then_inc(s_xn, 1)

            def x_lo(kt, count):
                dve.wait_ge(s_xT_hi, count)
                dve.tensor_tensor(xnT[1][:, kt, :], (gbank, hbank)[kt][2][:],
                                  xnT[0][:, kt, :].bitcast(F32), ALU.subtract).then_inc(s_xT_lo, 1)

            def argument(n, j):
                dve.wait_ge(s_sq, n + 1)
                dve.scalar_tensor_tensor(th[j % 2][:], sq[j % 2][:], 1.0 / GELU_A,
                                         gbank[slot(j)][:], ALU.add, ALU.mult).then_inc(s_arg, 1)

            def gated(n, j, loop):
                dve.wait_ge(s_tanh, n + 1)
                after(dve.scalar_tensor_tensor(act_v[j % 2][:], th[j % 2][:], 1.0,
                                               gbank[slot(j)][:], ALU.add, ALU.mult), loop)
                dve.scalar_tensor_tensor(act_v[j % 2][:], act_v[j % 2][:], 0.5,
                                         hbank[slot(j)][:], ALU.mult, ALU.mult).then_inc(s_inter, 1)

            dve.memset(y[:], 0.0).then_inc(s_down_used, 1)

            dve.wait_ge(s_x, 16)
            for t in (0, 2):
                stats_of(x_in, t, None)
            moments()
            dve.wait_ge(s_rstd, 1)
            for t in (0, 2):
                last = standardise(xn, x_in, t)
            last.then_inc(s_xn, 1)
            for kt in range(KT):
                x_lo(kt, kt + 1)
            for j in range(2):
                argument(j, j)
                gated(j, j, None)
            per_step = NT + 6
            start = chain.value
            with dve.Fori(0, NCH) as c:
                base = c * NT
                loop = c * per_step
                for j, (kind, m) in order:
                    if kind == "xT":
                        for kt in range(KT):
                            x_lo(kt, c * KT + (KT + kt + 1))
                    elif kind == "gu":
                        if m >= 2:
                            argument(base + m, m)
                            dve.wait_ge(s_iT_lo, base + (m - 1))
                            gated(base + m, m, loop)
                        if j < 6:
                            finish_y(j, c, loop)
                        elif 7 <= j < 11:
                            norm_next_x(j - 7, c, loop)
            assert chain.value - start == per_step
            for part in range(6):
                finish_y(part, NCH, NCH * per_step - per_step)

        @block.gpsimd
        def _(pool):
            pool.memset(power[:], -0.5).then_inc(s_pool, 1)
            pool.memset(ident[:], 0.0).then_inc(s_const, 1)
            pool.memset(token[:, 1:2], 0.0).then_inc(s_stored, 16)
            pool.wait_ge(s_const, 1)
            pool.affine_select(out=ident[:], in_=ident[:], compare_op=ALU.not_equal, fill=1.0,
                               base=0, pattern=[[-1, P]], channel_multiplier=1).then_inc(s_const, 1)
            chain = Tally(s_pool, 1)

            def roots(count, loop):
                pool.wait_ge(s_var, count)
                pool.sem_inc(s_pool_held, 1)
                chain.add(pool.tensor_scalar(var_eps[:], mv[:, :, 1], EPS, 1.0, ALU.add, ALU.mult))
                pool.wait_ge(s_pool, chain.value if loop is None else loop + chain.value)
                pool.tensor_tensor(rstd[:], var_eps[:], power[:], ALU.pow).then_inc(s_rstd, 1)

            def inter_lo(n, j):
                pool.wait_ge(s_iT_hi, n + 1)
                pool.tensor_tensor(iT[j % 4][1][:], act_v[j % 2][:], iT[j % 4][0][:].bitcast(F32),
                                   ALU.subtract).then_inc(s_iT_lo, 1)

            roots(1, None)
            inter_lo(0, 0)
            with pool.Fori(0, NCH) as c:
                base = c * NT
                for j, (kind, m) in order:
                    if kind == "gu":
                        inter_lo(base + (m - 1), m - 1)
                        if j == 1:
                            roots(c * 2 + 2, c * 2)
                        elif j == 8:
                            roots(c * 2 + 3, c * 2)
            roots(NCH * 2 + 2, NCH * 2 - 2)


def block_kernel(nc, x, w_pairs, bq, bk, bv, bo, words, scales, out):
    x_v = x.rearrange("b (t p) d -> p (b t) d", p=P)
    out_v = out.rearrange("b (t p) d -> p (b t) d", p=P)
    x1 = nc.dram_tensor("x1_scratch", (TOKENS + CHUNK, D), F32, kind="Internal").ap()
    x1_v = x1.rearrange("(t p) d -> p t d", p=P)
    w4_v = [nc.dram_tensor(f"w4_{s}_scratch", (P, PIECES, 2, P), F32, kind="Internal").ap()
            for s in ("hi", "lo")]
    attention_phase(nc, x_v, w_pairs, bq, bk, bv, bo, words, scales, x1_v, w4_v)
    mlp_phase(nc, x1_v[:, TT:, :], w4_v, out_v)


def kernel(**inputs):
    import numpy as _np
    import concourse.bacc as _bacc
    from concourse import mybir as _mybir
    from concourse.bass_utils import run_bass_kernel_spmd as _run

    nc = _bacc.Bacc("TRN2", target_bir_lowering=False, num_devices=1)
    given = {name.removeprefix("L0_"): _np.asarray(a) for name, a in inputs.items()}
    heads = {kind: given[f"attn_W_{kind.upper()}"] for kind in "qkvo"}
    for kind in "qkv":
        heads[kind] = heads[kind].reshape(HEADS, KT, P, E).transpose(0, 2, 1, 3)
    pairs = _np.stack([_np.stack([heads[kind][h].reshape(P, D) for kind, h in pair], axis=1)
                       for pair in PAIRS])
    q = NT // 2

    def columns(kind):
        gate, up = (given[f"ffn_{m}_{kind}"].reshape(q, P, 2, -1).transpose(3, 0, 2, 1)
                    for m in ("gate", "up"))
        down = given[f"ffn_down_{kind}"].reshape(2, P, q, -1).transpose(3, 2, 0, 1)
        gate_up = _np.stack([gate, up], axis=3).reshape(gate.shape[0], q, 4, P)
        pieces = _np.concatenate([gate_up, down], axis=2).reshape(gate.shape[0], PIECES * P)
        return _np.concatenate([pieces, pieces[:, :P]], axis=1)

    laid = {
        "x": _np.concatenate([given["attn_x"], given["attn_x"][:CHUNK // SEQ]]),
        "w_pairs": pairs,
        "b_Q": given["attn_b_Q"].T, "b_K": given["attn_b_K"].T, "b_V": given["attn_b_V"].T,
        "b_O": given["attn_b_O"],
        "words": columns("W_packed"), "scales": columns("scales"),
    }
    arrays, aps = {}, []
    for name, a in laid.items():
        a = _np.ascontiguousarray(a)
        arrays[f"in_{name}"] = a
        aps.append(nc.dram_tensor(f"in_{name}", a.shape, _mybir.dt.from_np(a.dtype),
                                  kind="ExternalInput").ap())
    out = nc.dram_tensor("out_0", (16, SEQ, D), _mybir.dt.float32, kind="ExternalOutput").ap()
    block_kernel(nc, *aps, out)
    r = _run(nc, [arrays], core_ids=[0])
    return r.results[0]["out_0"]
```

```python
import concourse.bass as bass
from concourse import mybir
from contextlib import ExitStack

F32 = mybir.dt.float32
F32R = mybir.dt.float32r
I32 = mybir.dt.int32
F16 = mybir.dt.float16
ALU = mybir.AluOpType
ACT = mybir.ActivationFunctionType

P = 128
D = 256
KT = D // P
HEADS = 16
E = 128
SEQ = 256
CHUNK = 512
TT = CHUNK // P
TOKENS = 16 * SEQ
NCH = TOKENS // CHUNK
HG = 4
EPS = 1e-5
MASKED = -100000.0 * float(E) ** 0.5
SCALE = float(E) ** -0.5
MLP = 2048
NT = MLP // P
BLK = 32
PIECES = 3 * NT
PPS = PIECES // NCH
GELU_C = 0.7978845608028654
GELU_A = 0.044715


class Tally:

    def __init__(self, sem, value=0):
        self.sem, self.value = sem, value

    def add(self, ins, by=1):
        ins.then_inc(self.sem, by)
        self.value += by
        return self.value


PAIRS = [pair for h in range(0, HEADS, HG) for pair in (
    (("q", h), ("k", h)), (("v", h), ("v", h + 1)), (("v", h + 2), ("v", h + 3)),
    (("q", h + 1), ("k", h + 1)), (("o", h), ("o", h + 1)), (("q", h + 2), ("k", h + 2)),
    (("q", h + 3), ("k", h + 3)), (("o", h + 2), ("o", h + 3)))]


class Shared:

    def __init__(self, nc, ctx):
        def sb(name, shape, dt=F32):
            return ctx.enter_context(nc.sbuf_tensor(name, shape, dt))

        self.ident = sb("ident", [P, P])
        self.power = sb("power", [P, TT])
        self.stream = sb("stream", [P, TT, D])
        self.x_res = sb("x_res", [P, TT, D])
        self.xnT = [sb(f"xnT_{s}", [P, KT, CHUNK], F32R) for s in ("hi", "lo")]


def attention_phase(nc, shared, x_v, w_pairs, bq, bk, bv, bo, words_v, scales_v, x1_v, w4_v):
    with ExitStack() as ctx:
        def sb(name, shape, dt=F32):
            return ctx.enter_context(nc.sbuf_tensor(name, shape, dt))

        def sem(name):
            return ctx.enter_context(nc.semaphore(name))

        wqk_p = [sb(f"wqk_{s}", [P, HEADS, 2, KT, E], F32R) for s in ("hi", "lo")]
        wv_p = [sb(f"wv_{s}", [P, HEADS, KT, E], F32R) for s in ("hi", "lo")]
        wo_p = [sb(f"wo_{s}", [P, HEADS, D], F32R) for s in ("hi", "lo")]
        RAW = 2
        raw = sb("w_raw", [P, RAW, 2, D])
        bias_q = sb("bias_q", [P, HEADS])
        bias_k = sb("bias_k", [P, HEADS])
        bias_v = sb("bias_v", [P, HEADS])
        bias_o = sb("bias_o", [P, D])
        mask = sb("mask", [P, SEQ])
        ident, power = shared.ident, shared.power
        x_in = sb("x_in", [P, TT, D])
        x_res = shared.x_res
        xn = shared.stream
        xnT = shared.xnT
        qT = [[sb(f"qT{i}_{s}", [P, CHUNK], F32R) for s in ("hi", "lo")] for i in range(2)]
        k_both = [sb(f"kT{i}", [P, 2, CHUNK], F32R) for i in range(2)]
        kT = [[k[:, s, :] for s in range(2)] for k in k_both]
        v = [sb(f"v_{s}", [P, TT, HG * E], F32R) for s in ("hi", "lo")]
        probs = [sb(f"probs{b}", [P, 384]) for b in range(2)]
        pT = [[sb(f"pT{b}_{s}", [P, 384], F32R) for s in ("hi", "lo")] for b in range(2)]
        zT = [sb(f"zT_{s}", [P, CHUNK], F32R) for s in ("hi", "lo")]
        words = sb("words", [P, P], I32)
        spread = sb("spread", [P, P], I32)
        scale = sb("scale", [P, P])
        w4 = sb("w4", [P, 2, P])
        w4_p = [[sb(f"w4_{i}{s}", [P, 2, P], F32R) for s in ("hi", "lo")] for i in range(2)]
        nmax = [[sb(f"nmax{i}{b}", [P, 2]) for b in range(2)] for i in range(2)]
        sums = [[sb(f"sums{i}{b}", [P, 2]) for b in range(2)] for i in range(2)]
        rsum = [[sb(f"rsum{i}{b}", [P, 2]) for b in range(2)] for i in range(2)]
        stats = sb("stats", [P, TT, 6])
        mv = sb("mv", [P, TT, 2])
        var_eps = sb("var_eps", [P, TT])
        rstd = sb("rstd", [P, TT])
        token = sb("token", [P, 2])

        FB, UB = 3, 3
        fbank = [ctx.enter_context(nc.psum_tensor(f"fbank{i}", [P, 512], F32)) for i in range(FB)]
        ubank = [ctx.enter_context(nc.psum_tensor(f"ubank{i}", [P, 512], F32)) for i in range(UB)]
        obank = [ctx.enter_context(nc.psum_tensor(f"obank{i}", [P, 2, D], F32)) for i in range(2)]

        s_w = [sem(f"w_loaded{i}") for i in range(RAW)]
        s_w_split = sem("w_split")
        s_bias = sem("bias_loaded")
        s_words = sem("words_loaded")
        s_w4 = sem("w4_dequantised")
        s_w4_hi = sem("w4_hi")
        s_w4_lo = sem("w4_lo")
        s_w4_stored = sem("w4_stored")
        s_const = sem("const_ready")
        s_x = sem("x_loaded")
        s_xres = sem("x_res_loaded")
        s_res_used = sem("residual_added")
        s_stored = sem("x1_stored")
        s_var = sem("variance_ready")
        s_rstd = sem("rstd_ready")
        s_pool = sem("pool_chain")
        s_xn = sem("xn_ready")
        s_full = sem("full_ready")
        s_hi = sem("full_hi")
        s_lo = sem("full_lo")
        s_scores = sem("scores_ready")
        s_masked = sem("masked_ready")
        s_exp = sem("exp_ready")
        s_rsum = sem("sums_inverted")
        s_probs = sem("probs_ready")
        s_pT = sem("pT_ready")
        s_pT_hi = sem("pT_hi")
        s_pT_lo = sem("pT_lo")
        s_out = sem("out_ready")
        s_out_used = sem("out_evacuated")
        s_dve_held = sem("dve_held")
        s_pool_held = sem("pool_held")
        s_dve = sem("dve_chain")

        def parts_of(pair):
            (kind, h), (other, _) = pair
            if kind == "q":
                return [p[:, h].rearrange("p m k e -> p m (k e)") for p in wqk_p]
            if kind == "v":
                return [p[:, h:h + 2].rearrange("p h k e -> p h (k e)") for p in wv_p]
            return [p[:, h:h + 2] for p in wo_p]

        def split_count(kind, h):
            return 1 + [(kind, h) in pair for pair in PAIRS].index(True)

        W4_SLOTS = [1, 3, 5, 7, 9, 11]
        X1_ROOTS, NEXT_ROOTS = 3, 11
        extras = {
            (0, "sum"): ("x1", 0), (2, "sum"): ("x1", 1), (2, "z"): ("x1", 2),
            (4, "masked"): ("x1", 3), (4, "sum"): ("x1", 4), (6, "sum"): ("x1", 5), (6, "z"): ("x1", 6),
            (8, "sum"): ("next", 0), (10, "sum"): ("next", 1), (10, "z"): ("next", 2),
            (12, "masked"): ("next", 3), (12, "sum"): ("next", 4),
        }
        for k, at in enumerate(W4_SLOTS):
            extras[at, "masked"] = ("spread0", k)
            extras[at, "sum"] = ("spread1", k)
            extras[at, "z"] = ("scaled", k)
        assert len(W4_SLOTS) == PPS

        FPC = 2 * HEADS + HEADS + (HEADS // HG) * TT + KT
        assert FPC % FB == 0
        UPC = 2 * HEADS
        FULL0 = KT + 2

        def step_plan(j):
            plan = [("q", j + 1), ("k", j + 1), ("pT", j)]
            if j == HEADS - 2:
                plan += [("xT", 0)]
            if j % HG == 0:
                plan += [("v", t) for t in range(TT)]
            if j > 0:
                plan += [("out", j - 1)]
            if j == HEADS - 2:
                plan += [("xT", 1)]
            if j < HEADS - 1:
                return plan + [("scores", j + 1), ("z", j)]
            return plan + [("z", j), ("scores", j + 1), ("out", j)]

        FULLS = ("q", "k", "v", "z", "xT")
        order = [(j, what) for j in range(HEADS) for what in step_plan(j)]
        place = {}
        for j, what in order:
            if what[0] in FULLS:
                group = j // HG if what[0] == "v" else 0
                place[what + (group,)] = len(place)
        assert len(place) == FPC

        def full_index(kind, n, group=0):
            return place[(kind, n, group)]

        block = ctx.enter_context(nc.Block())

        @block.sync
        def _(sp):
            def next_x(c, src):
                sp.wait_ge(s_xn, c + 1)
                sp.dma_start(x_in[:], src).then_inc(s_x, 16)

            def finish(c):
                sp.wait_ge(s_res_used, c * 2 + 2)
                sp.dma_start(x1_v[:, bass.ds(c * TT, TT), :], xn[:]).then_inc(s_stored, 16)
                sp.dma_start(x_res[:], x_v[:, bass.ds(c * TT, TT), :]).then_inc(s_xres, 16)

            sp.dma_start(x_in[:], x_v[:, 0:TT, :]).then_inc(s_x, 16)
            for n in range(len(PAIRS)):
                if n >= RAW:
                    sp.wait_ge(s_w_split, n - RAW + 1)
                sp.dma_start(raw[:, n % RAW], w_pairs[n]).then_inc(s_w[n % RAW], 16)
                if n == RAW - 1:
                    for dst, src in ((bias_q, bq), (bias_k, bk), (bias_v, bv)):
                        sp.dma_start(dst[:], src[:, :]).then_inc(s_bias, 16)
                    sp.dma_start(bias_o[:], bo.partition_broadcast(P)).then_inc(s_bias, 16)
                    sp.dma_start(x_res[:], x_v[:, 0:TT, :]).then_inc(s_xres, 16)
                if n == len(PAIRS) // 8:
                    next_x(0, x_v[:, TT:2 * TT, :])
                if n == 3 * len(PAIRS) // 4:
                    finish(0)
            with sp.Fori(1, NCH - 1) as c:
                next_x(c, x_v[:, bass.ds((c + 1) * TT, TT), :])
                finish(c)
            sp.wait_ge(s_stored, 32)
            next_x(NCH - 1, x1_v[:, TT:2 * TT, :])
            finish(NCH - 1)
            sp.wait_ge(s_stored, NCH * 16)
            sp.wait_ge(s_xres, (NCH + 1) * 16)

        @block.scalar
        def _(act):
            def split_hi(dst, bank, bias=None):
                if bias is None:
                    return act.activation(dst, bank, ACT.Copy)
                return act.activation(dst, bank, ACT.Identity, bias=bias)

            def full(n, dst, bank, bias=None):
                act.wait_ge(s_full, n + 1)
                split_hi(dst, bank, bias).then_inc(s_hi, 1)

            def exps(u, i, b):
                act.wait_ge(s_masked, u + 1)
                pr = probs[b]
                act.activation(pr[:, 0:P], pr[:, 0:P], ACT.Exp, bias=nmax[i][b][:, 0:1],
                               scale=-1.0, accum_out=sums[i][b][:, 0:1])
                act.activation(pr[:, P:384], pr[:, P:384], ACT.Exp, bias=nmax[i][b][:, 1:2],
                               scale=-1.0, accum_out=sums[i][b][:, 1:2]).then_inc(s_exp, 1)

            for kt in range(KT):
                full(kt, xnT[0][:, kt, :], fbank[kt % FB][:])
            act.wait_ge(s_bias, 64)
            full(KT, qT[0][0][:], fbank[KT % FB][:], bias_q[:, 0:1])
            full(KT + 1, kT[0][0][:], fbank[(KT + 1) % FB][:], bias_k[:, 0:1])
            for b in range(2):
                exps(b, 0, b)
            def w4_store(n, k):
                act.wait_ge(s_w4_lo, n + 2)
                for part in range(2):
                    act.dma_start(w4_v[part][:, bass.ds(n, 1)],
                                  w4_p[k % 2][part][:].bitcast(F32).unsqueeze(1)).then_inc(s_w4_stored, 16)

            def w4_hi(n, k):
                act.wait_ge(s_w4, n + 1)
                act.wait_ge(s_w4_stored, n * 32 + 32)
                act.activation(w4_p[k % 2][0][:], w4[:], ACT.Copy).then_inc(s_w4_hi, 1)

            def w4_load(n):
                act.dma_start(words[:], words_v[:, bass.ds(n * P, P)]).then_inc(s_words, 16)
                act.dma_start(scale[:], scales_v[:, bass.ds(n * P, P)].unsqueeze(1).broadcast_to(
                    [P // 16, 16, P])).then_inc(s_words, 16)

            w4_load(0)
            with act.Fori(0, NCH) as c:
                for j, what in order:
                    kind, m = what
                    if kind in FULLS:
                        i = full_index(kind, m, j // HG if kind == "v" else 0)
                        bank = fbank[(FULL0 + i) % FB][:]
                        n = c * FPC + (FULL0 + i)
                        h = m % HEADS
                        if kind == "q":
                            full(n, qT[h % 2][0][:], bank, bias_q[:, h:h + 1])
                        elif kind == "k":
                            full(n, kT[h % 2][0][:], bank, bias_k[:, h:h + 1])
                        elif kind == "v":
                            full(n, v[0][:, m, :], bank)
                        elif kind == "z":
                            full(n, zT[0][:], bank, bias_v[:, h:h + 1])
                        else:
                            full(n, xnT[0][:, m, :], bank)
                    elif kind == "pT":
                        for b in range(2):
                            u = 2 * m + b
                            act.wait_ge(s_pT, c * UPC + (u + 1))
                            split_hi(pT[b][0][:], ubank[u % UB][:, 0:384]).then_inc(s_pT_hi, 1)
                        for k, at in enumerate(W4_SLOTS):
                            if j == at + 2:
                                w4_store(c * PPS + k, k)
                        for k, at in enumerate(W4_SLOTS):
                            if j == at + 1:
                                w4_hi(c * PPS + k, k)
                                w4_load(c * PPS + (k + 1))
                    elif kind == "scores":
                        for b in range(2):
                            exps(c * UPC + (2 * m + b), m % 2, b)
            act.wait_ge(s_w4_stored, (PIECES + 2 - 1) * 32)
            act.wait_ge(s_words, (PIECES + 1) * 32)

        @block.tensor
        def _(pe):
            def three(out, a, b, start, stop, skip=False):
                nc.tensor.matmul(out, a[0], b[0], start=start, stop=False, skip_group_check=skip)
                nc.tensor.matmul(out, a[0], b[1], start=False, stop=False, skip_group_check=skip)
                return nc.tensor.matmul(out, a[1], b[0], start=False, stop=stop,
                                        skip_group_check=skip)

            def bank_free(n):
                pe.wait_ge(s_lo, n - FB + 1)

            def project(n, bank, h, which):
                bank_free(n)
                for kt in range(KT):
                    last = three(bank, [p[:, h, which, kt, :] for p in wqk_p],
                                 [p[:, kt, :] for p in xnT], kt == 0, kt == KT - 1)
                last.then_inc(s_full, 1)

            def transpose_x(n, kt, bank):
                for t in range(TT):
                    last = nc.tensor.transpose(bank[:, t * P:(t + 1) * P],
                                               xn[:, t, kt:D:KT], ident[:])
                last.then_inc(s_full, 1)

            def scores(i, b, bank):
                q, k = qT[i], kT[i]
                o = b * SEQ
                nc.tensor.matmul(bank[:].rearrange("p (r e) -> p r e", e=P)[:, 0:4:3, :],
                                 q[0][:, o:o + P], k_both[i][:, :, o:o + P],
                                 start=True, stop=False, skip_group_check=True)
                nc.tensor.matmul(bank[:, 0:P], q[1][:, o:o + P], k[0][:, o:o + P],
                                 start=False, stop=True, skip_group_check=True)
                three(bank[:, P:384], [p[:, o + P:o + SEQ] for p in q],
                      [p[:, o:o + SEQ] for p in k], True, True).then_inc(s_scores, 1)

            pe.wait_ge(s_const, 3)
            pe.wait_ge(s_xn, 1)
            for kt in range(KT):
                transpose_x(kt, kt, fbank[kt % FB])
            pe.wait_ge(s_lo, KT)
            pe.wait_ge(s_w_split, split_count("k", 0))
            for m in range(2):
                n = KT + m
                if n >= FB:
                    bank_free(n)
                for kt in range(KT):
                    last = three(fbank[n % FB][:], [p[:, 0, m, kt, :] for p in wqk_p],
                                 [p[:, kt, :] for p in xnT], kt == 0, kt == KT - 1)
                last.then_inc(s_full, 1)
            pe.wait_ge(s_lo, KT + 2)
            for b in range(2):
                scores(0, b, ubank[b])

            with pe.Fori(0, NCH) as c:
                base = c * FPC
                for j, what in order:
                    kind, m = what
                    if kind in FULLS:
                        i = full_index(kind, m, j // HG if kind == "v" else 0)
                        bank = fbank[(FULL0 + i) % FB]
                        n = base + (FULL0 + i)
                    h = m % HEADS
                    if kind in ("q", "k"):
                        if kind == "q" and m < HEADS:
                            pe.wait_ge(s_w_split, split_count("k", m))
                        if kind == "q" and m == HEADS:
                            pe.wait_ge(s_lo, base + (FULL0 + full_index("xT", KT - 1) + 1))
                        project(n, bank[:], h, 0 if kind == "q" else 1)
                    elif kind == "xT":
                        bank_free(n)
                        if m == 0:
                            pe.wait_ge(s_xn, c + 2)
                        transpose_x(n, m, bank)
                    elif kind == "v":
                        if m == 0:
                            pe.wait_ge(s_w_split, split_count("v", j + HG - 1))
                        bank_free(n)
                        for kt in range(KT):
                            last = three(bank[:].rearrange("p (h e) -> p h e", h=HG),
                                         [p[:, kt, m * P:(m + 1) * P] for p in xnT],
                                         [p[:, j:j + HG, kt, :] for p in wv_p],
                                         kt == 0, kt == KT - 1)
                        last.then_inc(s_full, 1)
                    elif kind == "scores":
                        pe.wait_ge(s_lo, base + (FULL0 + full_index("k", m) + 1))
                        for b in range(2):
                            u = 2 * m + b
                            if m == HEADS:
                                pe.wait_ge(s_pT_lo, c * UPC + (UPC - 1 + b))
                            elif u >= UB:
                                pe.wait_ge(s_pT_lo, c * UPC + (u - UB + 1))
                            scores(h % 2, b, ubank[(u % UPC) % UB])
                    elif kind == "pT":
                        for b in range(2):
                            u = 2 * m + b
                            bank = ubank[u % UB]
                            pr = probs[b]
                            pe.wait_ge(s_probs, c * UPC + (u + 1))
                            nc.tensor.transpose(bank[:, 0:P], pr[:, 0:P], ident[:])
                            nc.tensor.transpose(bank[:, P:2 * P], pr[:, P:2 * P], ident[:])
                            nc.tensor.transpose(bank[:, 2 * P:384], pr[:, 2 * P:384],
                                                ident[:]).then_inc(s_pT, 1)
                    elif kind == "z":
                        bank_free(n)
                        if m % HG == 0:
                            pe.wait_ge(s_lo, base + (FULL0 + full_index("v", TT - 1, m // HG) + 1))
                        e0 = (m % HG) * E
                        for b in range(2):
                            pe.wait_ge(s_pT_lo, c * UPC + (2 * m + b + 1))
                            o = b * SEQ
                            three(bank[:, o:o + SEQ], [p[:, 2 * b, e0:e0 + E] for p in v],
                                  [p[:, 0:SEQ] for p in pT[b]], True, False)
                            last = three(bank[:, o + P:o + SEQ],
                                         [p[:, 2 * b + 1, e0:e0 + E] for p in v],
                                         [p[:, SEQ:384] for p in pT[b]], False, True)
                        last.then_inc(s_full, 1)
                    elif kind == "out":
                        pe.wait_ge(s_lo, base + (FULL0 + full_index("z", m) + 1))
                        if m == 0:
                            pe.wait_ge(s_out_used, c + 1)
                        pe.wait_ge(s_w_split, split_count("o", m))
                        for t in range(TT):
                            last = three(obank[t // 2][:, t % 2, :],
                                         [p[:, t * P:(t + 1) * P] for p in zT],
                                         [p[:, m, :] for p in wo_p],
                                         m == 0 and t % 2 == 0, m == HEADS - 1, skip=True)
                        if m == HEADS - 1:
                            last.then_inc(s_out, 1)

        @block.vector
        def _(dve):
            chain = Tally(s_dve)

            def after(ins, loop=None):
                chain.add(ins)
                dve.wait_ge(s_dve, chain.value if loop is None else loop + chain.value)

            def full(n, dst, hi, bank, bias=None):
                dve.wait_ge(s_hi, n + 1)
                if bias is None:
                    ins = dve.tensor_tensor(dst, bank, hi.bitcast(F32), ALU.subtract)
                else:
                    ins = dve.scalar_tensor_tensor(dst, bank, bias, hi.bitcast(F32),
                                                   ALU.add, ALU.subtract)
                ins.then_inc(s_lo, 1)

            def mask_scores(u, i, b, bank, loop):
                dve.wait_ge(s_scores, u + 1)
                chain.add(dve.tensor_tensor(probs[b][:, 0:P], bank[:, 384:512], mask[:, P:SEQ],
                                            ALU.add))
                for lo, hi, part, added in ((P, 384, 1, mask[:]), (0, P, 0, probs[b][:, 0:P])):
                    if part == 0:
                        dve.wait_ge(s_dve, chain.value if loop is None else loop + chain.value)
                        dve.sem_inc(s_dve_held, 1)
                    last = dve.tensor_tensor_reduce(
                        out=probs[b][:, lo:hi], in0=bank[:, lo:hi], in1=added,
                        scale=-SCALE, scalar=3.0e38,
                        op0=ALU.add, op1=ALU.min, accum_out=nmax[i][b][:, part:part + 1])
                last.then_inc(s_masked, 1)

            def invert_sums(u, i, b):
                dve.wait_ge(s_exp, u + 1)
                dve.reciprocal(rsum[i][b][:], sums[i][b][:]).then_inc(s_rsum, 1)

            def stats_of(src, t, loop):
                for i in (t, t + 1):
                    last = dve.bn_stats(stats[:, i, :], src[:, i, :])
                after(last, loop)

            def moments():
                dve.sem_inc(s_dve_held, 1)
                for t in range(TT):
                    last = dve.bn_aggr(mv[:, t, :], stats[:, t, :])
                last.then_inc(s_var, 1)

            def standardise(dst, src, t):
                for i in (t, t + 1):
                    last = dve.tensor_scalar(dst[:, i, :], src[:, i, :], mv[:, i, 0:1],
                                             rstd[:, i:i + 1], ALU.subtract, ALU.mult)
                return last

            def finish_x1(part, c, loop):
                if part in (0, 1):
                    stats_of(xn, 2 * part, loop)
                elif part == 2:
                    moments()
                elif part in (3, 4):
                    dve.wait_ge(s_rstd, c * 2 + 2)
                    after(standardise(xn, xn, 2 * (part - 3)), loop)
                else:
                    t = 2 * (part - 5)
                    dve.wait_ge(s_xres, c * 16 + 16)
                    dve.tensor_tensor(xn[:, t:t + 2, :], xn[:, t:t + 2, :], x_res[:, t:t + 2, :],
                                      ALU.add).then_inc(s_res_used, 1)

            def norm_next_x(part, c, loop):
                if part in (0, 1):
                    dve.wait_ge(s_x, c * 16 + 32)
                    stats_of(x_in, 2 * part, loop)
                elif part == 2:
                    moments()
                elif part in (3, 4):
                    dve.wait_ge(s_rstd, c * 2 + 3)
                    dve.wait_ge(s_stored, c * 16 + 16)
                    last = standardise(xn, x_in, 2 * (part - 3))
                    if part == 4:
                        last.then_inc(s_xn, 1)

            def spread0(n, loop):
                dve.wait_ge(s_words, n * 32 + 32)
                after(dve.tensor_scalar(spread[:], words[:], 0xF0, 12, ALU.bitwise_and,
                                        ALU.logical_shift_left), loop)
                after(dve.scalar_tensor_tensor(spread[:], words[:], 0xF, spread[:],
                                               ALU.bitwise_and, ALU.bitwise_or), loop)

            def spread1(loop):
                dve.tensor_scalar(words[:], spread[:], 0x80008, 12, ALU.bitwise_and,
                                  ALU.logical_shift_left)
                after(dve.tensor_scalar(spread[:], spread[:], 0x70007, 9, ALU.bitwise_and,
                                        ALU.logical_shift_left), loop)
                after(dve.tensor_tensor(spread[:], spread[:], words[:], ALU.bitwise_or), loop)

            def scaled(n):
                dve.wait_ge(s_w4_lo, n + 1)
                pair = spread[:].bitcast(F16).rearrange("p (w r) -> p r w", r=2)
                for r in range(2):
                    last = dve.scalar_tensor_tensor(w4[:, r, :], pair[:, r, :], 16384.0,
                                                    scale[:], ALU.mult, ALU.mult)
                last.then_inc(s_w4, 1)

            def extra(j, place, c, loop):
                work, part = extras.get((j, place), (None, 0))
                if work == "x1":
                    finish_x1(part, c, loop)
                elif work == "next":
                    norm_next_x(part, c, loop)
                elif work == "spread0":
                    spread0(c * PPS + part, loop)
                elif work == "spread1":
                    spread1(loop)
                elif work == "scaled":
                    scaled(c * PPS + part)

            dve.memset(token[:, 0:1], 0.0).then_inc(s_out_used, 1)
            dve.wait_ge(s_x, 16)
            for t in (0, 2):
                stats_of(x_in, t, None)
            moments()
            dve.wait_ge(s_rstd, 1)
            for t in (0, 2):
                last = standardise(xn, x_in, t)
            last.then_inc(s_xn, 1)
            for kt in range(KT):
                full(kt, xnT[1][:, kt, :], xnT[0][:, kt, :], fbank[kt % FB][:])
            dve.wait_ge(s_bias, 64)
            full(KT, qT[0][1][:], qT[0][0][:], fbank[KT % FB][:], bias_q[:, 0:1])
            full(KT + 1, kT[0][1][:], kT[0][0][:], fbank[(KT + 1) % FB][:], bias_k[:, 0:1])
            dve.wait_ge(s_const, 3)
            for b in range(2):
                mask_scores(b, 0, b, ubank[b], None)
            for b in range(2):
                invert_sums(b, 0, b)

            per_step = 2 * HEADS + 6 + 4 * PPS
            start = chain.value
            with dve.Fori(0, NCH) as c:
                base = c * FPC
                loop = c * per_step
                for j, what in order:
                    kind, m = what
                    h = m % HEADS
                    if kind in FULLS:
                        i = full_index(kind, m, j // HG if kind == "v" else 0)
                        bank = fbank[(FULL0 + i) % FB][:]
                        n = base + (FULL0 + i)
                        if kind == "q":
                            full(n, qT[h % 2][1][:], qT[h % 2][0][:], bank, bias_q[:, h:h + 1])
                        elif kind == "k":
                            full(n, kT[h % 2][1][:], kT[h % 2][0][:], bank, bias_k[:, h:h + 1])
                        elif kind == "v":
                            full(n, v[1][:, m, :], v[0][:, m, :], bank)
                        elif kind == "z":
                            full(n, zT[1][:], zT[0][:], bank, bias_v[:, h:h + 1])
                            extra(j, "z", c, loop)
                        else:
                            full(n, xnT[1][:, m, :], xnT[0][:, m, :], bank)
                    elif kind == "pT":
                        for b in range(2):
                            u = 2 * m + b
                            dve.wait_ge(s_pT_hi, c * UPC + (u + 1))
                            dve.tensor_tensor(pT[b][1][:], ubank[u % UB][:, 0:384],
                                              pT[b][0][:].bitcast(F32),
                                              ALU.subtract).then_inc(s_pT_lo, 1)
                    elif kind == "scores":
                        for b in range(2):
                            u = 2 * m + b
                            mask_scores(c * UPC + u, h % 2, b, ubank[(u % UPC) % UB], loop)
                        extra(j, "masked", c, loop)
                        for b in range(2):
                            invert_sums(c * UPC + (2 * m + b), h % 2, b)
                            if b == 0:
                                extra(j, "sum", c, loop)
                dve.wait_ge(s_out, c + 1)
                for i in range(2):
                    last = dve.tensor_tensor(xn[:, 2 * i:2 * i + 2, :], obank[i][:],
                                             bias_o[:].unsqueeze(1).broadcast_to([P, 2, D]),
                                             ALU.add)
                last.then_inc(s_out_used, 1)
                dve.wait_ge(s_out_used, c + 2)
            assert chain.value - start == per_step, (chain.value, start)

        @block.gpsimd
        def _(pool):
            pool.memset(ident[:], 0.0).then_inc(s_pool, 1)
            pool.memset(mask[:], 0.0).then_inc(s_pool, 1)
            pool.memset(power[:], -0.5).then_inc(s_const, 1)
            pool.wait_ge(s_pool, 2)
            pool.affine_select(out=ident[:], in_=ident[:], compare_op=ALU.not_equal, fill=1.0,
                               base=0, pattern=[[-1, P]], channel_multiplier=1).then_inc(s_const, 1)
            pool.affine_select(out=mask[:, P:SEQ], in_=mask[:, P:SEQ], compare_op=ALU.is_ge,
                               fill=MASKED, base=0, pattern=[[-1, P]],
                               channel_multiplier=1).then_inc(s_const, 1)
            pool.wait_ge(s_const, 3)
            chain = Tally(s_pool, 2)

            def roots(count, loop):
                pool.wait_ge(s_var, count)
                pool.sem_inc(s_pool_held, 1)
                chain.add(pool.tensor_scalar(var_eps[:], mv[:, :, 1], EPS, 1.0, ALU.add, ALU.mult))
                pool.wait_ge(s_pool, chain.value if loop is None else loop + chain.value)
                pool.tensor_tensor(rstd[:], var_eps[:], power[:], ALU.pow).then_inc(s_rstd, 1)

            roots(1, None)
            def w4_lo(n, k):
                pool.wait_ge(s_w4_hi, n + 1)
                pool.tensor_tensor(w4_p[k % 2][1][:], w4[:], w4_p[k % 2][0][:].bitcast(F32),
                                   ALU.subtract).then_inc(s_w4_lo, 1)

            def normalise(u, i, b):
                pool.wait_ge(s_rsum, u + 1)
                pool.sem_inc(s_pool_held, 1)
                for lo, hi, part in ((0, P, 0), (P, 384, 1)):
                    last = pool.tensor_scalar(probs[b][:, lo:hi], probs[b][:, lo:hi],
                                              rsum[i][b][:, part:part + 1], 1.0,
                                              ALU.mult, ALU.mult)
                last.then_inc(s_probs, 1)

            def slot(c, j, loop):
                if j - 1 in W4_SLOTS:
                    w4_lo(c * PPS + W4_SLOTS.index(j - 1), W4_SLOTS.index(j - 1))
                for b in range(2):
                    normalise(c * UPC + (2 * (j + 1) + b), (j + 1) % 2, b)
                if j == X1_ROOTS:
                    roots(c * 2 + 2, loop)
                if j == NEXT_ROOTS:
                    roots(c * 2 + 3, loop)

            pool.memset(token[:, 0:1], 0.0).then_inc(s_w4_lo, 1)
            pool.memset(token[:, 1:2], 0.0).then_inc(s_w4_stored, 32)

            done = 0
            for n, pair in enumerate(PAIRS):
                pool.wait_ge(s_w[n % RAW], 16 * (n // RAW + 1))
                hi, lo = parts_of(pair)
                chain.add(pool.tensor_scalar(hi, raw[:, n % RAW], 1.0, 1.0, ALU.mult, ALU.mult))
                pool.wait_ge(s_pool, chain.value)
                last = pool.tensor_tensor(lo, raw[:, n % RAW], hi.bitcast(F32), ALU.subtract)
                last.then_inc(s_w_split, 1)
                if n == 4:
                    for b in range(2):
                        normalise(b, 0, b)
                if n >= 8 and n % 2 == 0:
                    slot(0, done, None)
                    done += 1
            for j in range(done, HEADS):
                slot(0, j, None)
            with pool.Fori(1, NCH) as c:
                for j in range(HEADS):
                    slot(c, j, (c - 1) * 2)


def mlp_phase(nc, shared, x1_v, w4_v, out_v):
    with ExitStack() as ctx:
        def sb(name, shape, dt=F32):
            return ctx.enter_context(nc.sbuf_tensor(name, shape, dt))

        def sem(name):
            return ctx.enter_context(nc.semaphore(name))

        w4 = [sb(f"w4all_{s}", [P, PIECES, 2, P], F32R) for s in ("hi", "lo")]
        ident, power = shared.ident, shared.power
        x_in = sb("x1_in", [P, TT, D])
        x_res, y = shared.x_res, shared.stream
        xn = sb("x1n", [P, TT, D])
        xnT = shared.xnT
        sq = [sb(f"sq{i}", [P, CHUNK]) for i in range(2)]
        th = [sb(f"th{i}", [P, CHUNK]) for i in range(2)]
        act_v = [sb(f"inter{i}", [P, CHUNK]) for i in range(2)]
        iT = [[sb(f"iT{i}_{s}", [P, CHUNK], F32R) for s in ("hi", "lo")] for i in range(4)]
        stats = sb("stats2", [P, TT, 6])
        mv = sb("mv2", [P, TT, 2])
        var_eps = sb("var_eps2", [P, TT])
        rstd = sb("rstd2", [P, TT])
        token = sb("token2", [P, 2])

        gbank = [ctx.enter_context(nc.psum_tensor(f"gbank{i}", [P, 512], F32)) for i in range(3)]
        hbank = [ctx.enter_context(nc.psum_tensor(f"hbank{i}", [P, 512], F32)) for i in range(3)]
        obank = [ctx.enter_context(nc.psum_tensor(f"dbank{i}", [P, 2, D], F32)) for i in range(2)]

        s_w4 = [sem(f"w4_loaded{q}") for q in range(NT // 2)]
        s_w4_first = sem("w4_first_loaded")
        s_pool = sem("pool2_chain")
        s_dve = sem("dve2_chain")
        s_dve_held = sem("dve2_held")
        s_pool_held = sem("pool2_held")
        s_x = sem("x1_loaded")
        s_xres = sem("x1_res_loaded")
        s_var = sem("variance2_ready")
        s_rstd = sem("rstd2_ready")
        s_xn = sem("x1n_ready")
        s_xT = sem("x1nT_ready")
        s_xT_hi = sem("x1nT_hi")
        s_xT_lo = sem("x1nT_lo")
        s_gate = sem("gate_ready")
        s_up = sem("up_ready")
        s_sq = sem("square_ready")
        s_arg = sem("tanh_argument_ready")
        s_tanh = sem("tanh_ready")
        s_inter = sem("inter_ready")
        s_iT_hi = sem("inter_hi")
        s_iT_lo = sem("inter_lo")
        s_down = sem("down_ready")
        s_down_used = sem("down_evacuated")
        s_y = sem("y_ready")
        s_stored = sem("out_stored")

        def slot(j):
            return 1 if j == NT - 1 else (j % NT) % 3

        def plan(j):
            if j == NT - 3:
                return [("gu", j + 2), ("xT", 0), ("down", j)]
            if j == NT - 2:
                return [("down", j), ("gu", j + 2)]
            return [("gu", j + 2), ("down", j)]

        order = [(j, what) for j in range(NT) for what in plan(j)]
        block = ctx.enter_context(nc.Block())

        @block.sync
        def _(sp):
            def load(n0, n1, loaded):
                for part in range(2):
                    sp.dma_start(w4[part][:, n0:n1].bitcast(F32),
                                 w4_v[part][:, n0:n1]).then_inc(loaded, 16)

            load(0, 2, s_w4_first)
            load(2, 6, s_w4[0])
            for q in range(1, NT // 2):
                load(q * 6, q * 6 + 6, s_w4[q])

            def look_ahead(c):
                sp.wait_ge(s_xn, c)
                sp.dma_start(x_in[:], x1_v[:, bass.ds((c + 1) * TT, TT), :]).then_inc(s_x, 16)

            def finish(c):
                sp.wait_ge(s_y, c + 1)
                sp.dma_start(out_v[:, bass.ds((c - 1) * TT, TT), :], y[:]).then_inc(s_stored, 16)

            def residual(c):
                sp.dma_start(x_res[:], x1_v[:, bass.ds(c * TT, TT), :]).then_inc(s_xres, 16)

            sp.dma_start(x_in[:], x1_v[:, TT:2 * TT, :]).then_inc(s_x, 16)
            sp.wait_ge(s_y, 1)
            sp.dma_start(x1_v[:, (NCH - 1) * TT:, :], y[:]).then_inc(s_stored, 16)
            residual(0)
            sp.wait_ge(s_stored, 16)
            with sp.Fori(1, NCH - 1) as c:
                look_ahead(c)
                finish(c)
                residual(c)
            sp.wait_ge(s_xn, NCH - 1)
            sp.dma_start(x_in[:], x1_v[:, 0:TT, :]).then_inc(s_x, 16)
            finish(NCH - 1)
            residual(NCH - 1)
            finish(NCH)
            sp.wait_ge(s_stored, 16 + NCH * 16)

        @block.scalar
        def _(act):
            def x_hi(kt, count):
                act.wait_ge(s_xT, count)
                act.activation(xnT[0][:, kt, :], (gbank, hbank)[kt][0][:],
                               ACT.Copy).then_inc(s_xT_hi, 1)

            def square(n, j):
                act.wait_ge(s_gate, n + 1)
                act.activation(sq[j % 2][:], gbank[slot(j)][:], ACT.Square).then_inc(s_sq, 1)

            def tanh(n, j):
                act.wait_ge(s_arg, n + 1)
                act.activation(th[j % 2][:], th[j % 2][:], ACT.Tanh,
                               scale=GELU_C * GELU_A).then_inc(s_tanh, 1)

            def inter_hi(n, j):
                act.wait_ge(s_inter, n + 1)
                act.activation(iT[j % 4][0][:], act_v[j % 2][:], ACT.Copy).then_inc(s_iT_hi, 1)

            square(0, 0)
            tanh(0, 0)
            square(1, 1)
            inter_hi(0, 0)
            tanh(1, 1)
            with act.Fori(0, NCH) as c:
                base = c * NT
                for j, (kind, m) in order:
                    if kind == "xT":
                        for kt in range(KT):
                            x_hi(kt, c * KT + (kt + 1))
                    elif kind == "gu":
                        square(base + m, m)
                        inter_hi(base + (m - 1), m - 1)
                        tanh(base + m, m)
                act.wait_ge(s_stored, c * 16 + 16)
                act.wait_ge(s_down, c + 1)
                for i in range(2):
                    last = act.activation(y[:, 2 * i:2 * i + 2, :], obank[i][:], ACT.Copy)
                last.then_inc(s_down_used, 1)

        @block.tensor
        def _(pe):
            def three(out, a, b, start, stop, skip=False):
                nc.tensor.matmul(out, a[0], b[0], start=start, stop=False, skip_group_check=skip)
                nc.tensor.matmul(out, a[0], b[1], start=False, stop=False, skip_group_check=skip)
                return nc.tensor.matmul(out, a[1], b[0], start=False, stop=stop,
                                        skip_group_check=skip)

            def transpose_x(count):
                pe.wait_ge(s_xn, count)
                for kt in range(KT):
                    bank = (gbank, hbank)[kt][0]
                    for t in range(TT):
                        last = nc.tensor.transpose(bank[:, t * P:(t + 1) * P],
                                                   xn[:, t, kt:D:KT], ident[:])
                    last.then_inc(s_xT, 1)

            def gate_up(j):
                i = j % NT
                if j == 0:
                    pe.wait_ge(s_w4_first, 32)
                elif i % 2 == 0 or j == 1:
                    pe.wait_ge(s_w4[i // 2], 32)
                for up, banks in ((0, gbank), (1, hbank)):
                    for kt in range(KT):
                        n = 6 * (i // 2) + 2 * (i % 2) + up
                        last = three(banks[slot(j)][:], [p[:, n, kt, :] for p in w4],
                                     [p[:, kt, :] for p in xnT], kt == 0, kt == KT - 1)
                    last.then_inc(s_up if up else s_gate, 1)

            gate_up(0)
            gate_up(1)
            with pe.Fori(0, NCH) as c:
                base = c * NT
                for j, (kind, m) in order:
                    if kind == "xT":
                        pe.wait_ge(s_inter, base + (NT - 3))
                        transpose_x(c + 1)
                    elif kind == "gu":
                        if m == NT:
                            pe.wait_ge(s_xT_lo, c * KT + KT)
                        elif m == NT + 1:
                            pe.wait_ge(s_inter, base + NT)
                        elif m == NT - 1:
                            pe.wait_ge(s_inter, base + (NT - 2))
                        elif 3 <= m < NT - 1:
                            pe.wait_ge(s_inter, base + (m - 2))
                        gate_up(m)
                    else:
                        pe.wait_ge(s_iT_hi, base + (m + 1))
                        pe.wait_ge(s_iT_lo, base + (m + 1))
                        if m == 0:
                            pe.wait_ge(s_down_used, c + 1)
                        for t in range(TT):
                            out = obank[t // 2][:, t % 2, :].rearrange("p (h e) -> p h e", e=P)
                            n = 6 * (m // 2) + 4
                            last = three(out, [p[:, t * P:(t + 1) * P] for p in iT[m % 4]],
                                         [p[:, n:n + 2, m % 2, :] for p in w4],
                                         m == 0 and t % 2 == 0, m == NT - 1, skip=True)
                        if m == NT - 1:
                            last.then_inc(s_down, 1)

        @block.vector
        def _(dve):
            chain = Tally(s_dve)

            def after(ins, loop=None):
                chain.add(ins)
                dve.wait_ge(s_dve, chain.value if loop is None else loop + chain.value)

            def stats_of(src, t, loop):
                for i in (t, t + 1):
                    last = dve.bn_stats(stats[:, i, :], src[:, i, :])
                after(last, loop)

            def moments():
                dve.sem_inc(s_dve_held, 1)
                for t in range(TT):
                    last = dve.bn_aggr(mv[:, t, :], stats[:, t, :])
                last.then_inc(s_var, 1)

            def standardise(dst, src, t):
                for i in (t, t + 1):
                    last = dve.tensor_scalar(dst[:, i, :], src[:, i, :], mv[:, i, 0:1],
                                             rstd[:, i:i + 1], ALU.subtract, ALU.mult)
                return last

            def finish_y(part, c, loop):
                if part in (0, 1):
                    dve.wait_ge(s_down_used, c + 1)
                    stats_of(y, 2 * part, loop)
                    if part == 1:
                        moments()
                elif part in (2, 3):
                    dve.wait_ge(s_rstd, c * 2 + 1)
                    after(standardise(y, y, 2 * (part - 2)), loop)
                else:
                    t = 2 * (part - 4)
                    dve.wait_ge(s_xres, c * 16 + 16)
                    last = dve.tensor_tensor(y[:, t:t + 2, :], y[:, t:t + 2, :],
                                             x_res[:, t:t + 2, :], ALU.add)
                    if part == 5:
                        last.then_inc(s_y, 1)

            def norm_next_x(part, c, loop):
                if part in (0, 1):
                    dve.wait_ge(s_x, c * 16 + 16)
                    stats_of(x_in, 2 * part, loop)
                    if part == 1:
                        moments()
                elif part in (2, 3):
                    dve.wait_ge(s_rstd, c * 2 + 2)
                    last = standardise(xn, x_in, 2 * (part - 2))
                    if part == 3:
                        last.then_inc(s_xn, 1)

            def x_lo(kt, count):
                dve.wait_ge(s_xT_hi, count)
                dve.tensor_tensor(xnT[1][:, kt, :], (gbank, hbank)[kt][0][:],
                                  xnT[0][:, kt, :].bitcast(F32), ALU.subtract).then_inc(s_xT_lo, 1)

            def argument(n, j):
                dve.wait_ge(s_sq, n + 1)
                dve.scalar_tensor_tensor(th[j % 2][:], sq[j % 2][:], 1.0 / GELU_A,
                                         gbank[slot(j)][:], ALU.add, ALU.mult).then_inc(s_arg, 1)

            def gated(n, j, loop):
                dve.wait_ge(s_tanh, n + 1)
                after(dve.scalar_tensor_tensor(act_v[j % 2][:], th[j % 2][:], 1.0,
                                               gbank[slot(j)][:], ALU.add, ALU.mult), loop)
                dve.wait_ge(s_up, n + 1)
                dve.scalar_tensor_tensor(act_v[j % 2][:], act_v[j % 2][:], 0.5,
                                         hbank[slot(j)][:], ALU.mult, ALU.mult).then_inc(s_inter, 1)

            dve.memset(token[:, 0:1], 0.0).then_inc(s_down_used, 1)
            for j in range(2):
                argument(j, j)
                gated(j, j, None)
            per_step = NT + 6
            start = chain.value
            with dve.Fori(0, NCH) as c:
                base = c * NT
                loop = c * per_step
                for j, (kind, m) in order:
                    if kind == "xT":
                        for kt in range(KT):
                            x_lo(kt, c * KT + (kt + 1))
                    elif kind == "gu":
                        if m >= 2:
                            argument(base + m, m)
                            dve.wait_ge(s_iT_lo, base + (m - 1))
                            gated(base + m, m, loop)
                        if j < 6:
                            finish_y(j, c, loop)
                        elif 7 <= j < 11:
                            norm_next_x(j - 7, c, loop)
            assert chain.value - start == per_step
            for part in range(6):
                finish_y(part, NCH, NCH * per_step - per_step)

        @block.gpsimd
        def _(pool):
            pool.memset(token[:, 1:2], 0.0).then_inc(s_xres, 16)
            chain = Tally(s_pool)

            def roots(count, loop):
                pool.wait_ge(s_var, count)
                pool.sem_inc(s_pool_held, 1)
                chain.add(pool.tensor_scalar(var_eps[:], mv[:, :, 1], EPS, 1.0, ALU.add, ALU.mult))
                pool.wait_ge(s_pool, chain.value if loop is None else loop + chain.value)
                pool.tensor_tensor(rstd[:], var_eps[:], power[:], ALU.pow).then_inc(s_rstd, 1)

            def inter_lo(n, j):
                pool.wait_ge(s_iT_hi, n + 1)
                pool.tensor_tensor(iT[j % 4][1][:], act_v[j % 2][:], iT[j % 4][0][:].bitcast(F32),
                                   ALU.subtract).then_inc(s_iT_lo, 1)

            inter_lo(0, 0)
            with pool.Fori(0, NCH) as c:
                base = c * NT
                for j, (kind, m) in order:
                    if kind == "gu":
                        inter_lo(base + (m - 1), m - 1)
                        if j == 1:
                            roots(c * 2 + 1, c * 2)
                        elif j == 8:
                            roots(c * 2 + 2, c * 2)
            roots(NCH * 2 + 1, NCH * 2 - 2)


def block_kernel(nc, x, w_pairs, bq, bk, bv, bo, words, scales, out):
    x_v = x.rearrange("b (t p) d -> p (b t) d", p=P)
    out_v = out.rearrange("b (t p) d -> p (b t) d", p=P)
    x1 = nc.dram_tensor("x1_scratch", (TOKENS + CHUNK, D), F32, kind="Internal").ap()
    x1_v = x1.rearrange("(t p) d -> p t d", p=P)
    w4_v = [nc.dram_tensor(f"w4_{s}_scratch", (P, PIECES, 2, P), F32, kind="Internal").ap()
            for s in ("hi", "lo")]
    with ExitStack() as ctx:
        shared = Shared(nc, ctx)
        attention_phase(nc, shared, x_v, w_pairs, bq, bk, bv, bo, words, scales, x1_v, w4_v)
        mlp_phase(nc, shared, x1_v[:, TT:, :], w4_v, out_v)


def kernel(**inputs):
    import numpy as _np
    import concourse.bacc as _bacc
    from concourse import mybir as _mybir
    from concourse.bass_utils import run_bass_kernel_spmd as _run

    nc = _bacc.Bacc("TRN2", target_bir_lowering=False, num_devices=1)
    given = {name.removeprefix("L0_"): _np.asarray(a) for name, a in inputs.items()}
    heads = {kind: given[f"attn_W_{kind.upper()}"] for kind in "qkvo"}
    for kind in "qkv":
        heads[kind] = heads[kind].reshape(HEADS, P, KT, E)
    pairs = _np.stack([_np.stack([heads[kind][h].reshape(P, D) for kind, h in pair], axis=1)
                       for pair in PAIRS])
    q = NT // 2

    def columns(kind):
        gate, up = (given[f"ffn_{m}_{kind}"].reshape(q, P, 2, -1).transpose(3, 0, 2, 1)
                    for m in ("gate", "up"))
        down = given[f"ffn_down_{kind}"].reshape(2, P, q, -1).transpose(3, 2, 0, 1)
        gate_up = _np.stack([gate, up], axis=3).reshape(gate.shape[0], q, 4, P)
        pieces = _np.concatenate([gate_up, down], axis=2).reshape(gate.shape[0], PIECES * P)
        return _np.concatenate([pieces, pieces[:, :P]], axis=1)

    laid = {
        "x": given["attn_x"],
        "w_pairs": pairs,
        "b_Q": given["attn_b_Q"].T, "b_K": given["attn_b_K"].T, "b_V": given["attn_b_V"].T,
        "b_O": given["attn_b_O"],
        "words": columns("W_packed"), "scales": columns("scales"),
    }
    arrays, aps = {}, []
    for name, a in laid.items():
        a = _np.ascontiguousarray(a)
        arrays[f"in_{name}"] = a
        aps.append(nc.dram_tensor(f"in_{name}", a.shape, _mybir.dt.from_np(a.dtype),
                                  kind="ExternalInput").ap())
    out = nc.dram_tensor("out_0", (16, SEQ, D), _mybir.dt.float32, kind="ExternalOutput").ap()
    block_kernel(nc, *aps, out)
    r = _run(nc, [arrays], core_ids=[0])
    return r.results[0]["out_0"]
```
